# Optimizing a Trainium2 kernel written in Bass

```python
import numpy as np
import jax
import jax.numpy as jnp

def _softmax(x, axis=-1):
    return jax.nn.softmax(x, axis=axis)

def _gelu(x):
    return jax.nn.gelu(x, approximate=True)

def _silu(x):
    return jax.nn.silu(x)

def _sigmoid(x):
    return jax.nn.sigmoid(x)

def _layernorm(x, axis=-1, eps=1e-05):
    m = jnp.mean(x, axis=axis, keepdims=True)
    v = jnp.var(x, axis=axis, keepdims=True)
    return (x - m) / jnp.sqrt(v + eps)

def _scatter_add(tgt, idx, src, axis=0):
    return tgt.at[idx].add(src)

def _segment_sum(src, seg, n):
    return jax.ops.segment_sum(src, seg, n)
kernel_name = 'mk_decoder_preln_d1_seqx_r8_47f560'

def setup_inputs(seed: int=0):
    np.random.seed(seed)
    _w = jnp.asarray

    def _rec_inputs():
        import jax
        import jax.numpy as jnp
        _rk = jax.random.key(seed)
        x = 7.22e-05 + 1 * jax.random.normal(jax.random.fold_in(_rk, 1), (8, 256, 128), jnp.float32)
        _lenS = 256 - jax.random.randint(jax.random.fold_in(_rk, 7), (8,), 0, max(1, 256 // 4) + 1, jnp.int32)
        _lenS2 = 256 - jax.random.randint(jax.random.fold_in(_rk, 8), (8,), 0, max(1, 256 // 4) + 1, jnp.int32)
        _ctx_1024P = jax.random.normal(jax.random.fold_in(_rk, 11), (8, 16, 128), jnp.float32)
        _ctx_1024c = jax.random.dirichlet(jax.random.fold_in(_rk, 511), 0.3 * jnp.ones((16,), jnp.float32), (8, 256))
        _ctx_1024t = jnp.einsum('bsk,bkd->bsd', _ctx_1024c, _ctx_1024P)
        _ctx_1024t = _ctx_1024t * jax.lax.rsqrt(jnp.mean(jnp.square(_ctx_1024t)) + 1e-12) * 0.953939
        ctx_1024 = 4.13588e-05 + 0.999923 * (_ctx_1024t + 0.3 * jax.random.normal(jax.random.fold_in(_rk, 611), (8, 256, 128), jnp.float32))
        return (x, ctx_1024)
    x, ctx_1024 = _rec_inputs()

    def _L0_attn_setup():
        import jax, jax.numpy as jnp
        import numpy as np
        B, T, C = (4, 512, 128)
        H = 16
        D = C // H
        EPS = 1e-06

        def _phi(x):
            return jax.nn.elu(x) + 1.0
        key = jax.random.key(seed)
        k1, k2, k3 = jax.random.split(key, 3)
        x = jax.random.normal(k1, (B, T, C), dtype=jnp.float32)
        Wqkv = jax.random.normal(k2, (3 * C, C), dtype=jnp.float32) * (1.0 / np.sqrt(C))
        Wproj = jax.random.normal(k3, (C, C), dtype=jnp.float32) * (1.0 / np.sqrt(C))
        bproj = jnp.zeros((C,), dtype=jnp.float32)
        return {'x': x, 'Wqkv': Wqkv, 'Wproj': Wproj, 'bproj': bproj}
    _L0_attn_all = _L0_attn_setup()
    _L0_attn_in = {k: v for k, v in _L0_attn_all.items() if k in ('Wqkv', 'Wproj', 'bproj')}
    del _L0_attn_all

    def _L0_xattn_setup():
        import jax, jax.numpy as jnp
        import numpy as np
        D_MODEL = 128
        N_HEADS = 16
        HEAD_DIM = D_MODEL // N_HEADS
        key = jax.random.key(seed)
        ks = jax.random.split(key, 6)
        B, S = (4, 256)
        query = jax.random.normal(ks[0], (B, S, D_MODEL), dtype=jnp.float32)
        key_value = jax.random.normal(ks[1], (B, S, D_MODEL), dtype=jnp.float32)
        scale = 1.0 / np.sqrt(D_MODEL)
        Wq = jax.random.normal(ks[2], (D_MODEL, D_MODEL), dtype=jnp.float32) * scale
        Wk = jax.random.normal(ks[3], (D_MODEL, D_MODEL), dtype=jnp.float32) * scale
        Wv = jax.random.normal(ks[4], (D_MODEL, D_MODEL), dtype=jnp.float32) * scale
        Wo = jax.random.normal(ks[5], (D_MODEL, D_MODEL), dtype=jnp.float32) * scale
        return {'query': query, 'key_value': key_value, 'Wq': Wq, 'Wk': Wk, 'Wv': Wv, 'Wo': Wo}
    _L0_xattn_all = _L0_xattn_setup()
    _L0_xattn_in = {k: v for k, v in _L0_xattn_all.items() if k in ('Wq', 'Wk', 'Wv', 'Wo')}
    del _L0_xattn_all

    def _L0_ffn_setup():
        import jax, jax.numpy as jnp
        import numpy as np
        from jax import lax
        H = 128
        E = 8
        E_MLP = E - 4
        TOP_K = 2
        I = 64
        KC = 4
        SHARED_SCALE = 1.0
        key = jax.random.key(seed)
        ks = jax.random.split(key, 8)
        B, S = (4, 512)
        s_h = 1.0 / np.sqrt(H)
        s_i = 1.0 / np.sqrt(I)
        return {'hidden_states': jax.random.normal(ks[0], (B, S, H), dtype=jnp.float32), 'Wr': jax.random.normal(ks[1], (H, E), dtype=jnp.float32) * s_h, 'router_bias': jnp.zeros((E,), dtype=jnp.float32), 'Wg': jax.random.normal(ks[2], (E_MLP, H, I), dtype=jnp.float32) * s_h, 'Wu': jax.random.normal(ks[3], (E_MLP, H, I), dtype=jnp.float32) * s_h, 'Wd': jax.random.normal(ks[4], (E_MLP, I, H), dtype=jnp.float32) * s_i, 'conv_w': jax.random.normal(ks[5], (KC, 1, H), dtype=jnp.float32) * (1.0 / np.sqrt(KC)), 'conv_b': jnp.zeros((H,), dtype=jnp.float32)}
    _L0_ffn_all = _L0_ffn_setup()
    _L0_ffn_in = {k: v for k, v in _L0_ffn_all.items() if k in ('Wr', 'router_bias', 'Wg', 'Wu', 'Wd', 'conv_w', 'conv_b')}
    del _L0_ffn_all
    return {'x': x, 'ctx_1024': ctx_1024, 'L0_attn_Wqkv': _L0_attn_in['Wqkv'], 'L0_attn_Wproj': _L0_attn_in['Wproj'], 'L0_attn_bproj': _L0_attn_in['bproj'], 'L0_xattn_Wq': _L0_xattn_in['Wq'], 'L0_xattn_Wk': _L0_xattn_in['Wk'], 'L0_xattn_Wv': _L0_xattn_in['Wv'], 'L0_xattn_Wo': _L0_xattn_in['Wo'], 'L0_ffn_Wr': _L0_ffn_in['Wr'], 'L0_ffn_router_bias': _L0_ffn_in['router_bias'], 'L0_ffn_Wg': _L0_ffn_in['Wg'], 'L0_ffn_Wu': _L0_ffn_in['Wu'], 'L0_ffn_Wd': _L0_ffn_in['Wd'], 'L0_ffn_conv_w': _L0_ffn_in['conv_w'], 'L0_ffn_conv_b': _L0_ffn_in['conv_b']}

def reference(x, ctx_1024, L0_attn_Wqkv, L0_attn_Wproj, L0_attn_bproj, L0_xattn_Wq, L0_xattn_Wk, L0_xattn_Wv, L0_xattn_Wo, L0_ffn_Wr, L0_ffn_router_bias, L0_ffn_Wg, L0_ffn_Wu, L0_ffn_Wd, L0_ffn_conv_w, L0_ffn_conv_b):
    import jax
    import jax.numpy as jnp

    def _L0_attn_ref(x, Wqkv, Wproj, bproj):
        import jax, jax.numpy as jnp
        import numpy as np
        B, T, C = (4, 512, 128)
        H = 16
        D = C // H
        EPS = 1e-06

        def _phi(x):
            return jax.nn.elu(x) + 1.0
        b, t, c = x.shape
        qkv = jnp.einsum('btc,ec->bte', x, Wqkv)
        qkv = qkv.reshape(b, t, 3, H, D)
        q, k, v = (qkv[:, :, 0], qkv[:, :, 1], qkv[:, :, 2])
        q = _phi(q)
        k = _phi(k)
        kv = jnp.einsum('bnhd,bnhm->bhdm', k, v)
        k_sum = k.sum(axis=1)
        out = jnp.einsum('bnhd,bhdm->bnhm', q, kv)
        normalizer = jnp.einsum('bnhd,bhd->bnh', q, k_sum) + EPS
        out = out / normalizer[..., None]
        out = out.reshape(b, t, c)
        out = jnp.einsum('btc,oc->bto', out, Wproj) + bproj
        return out

    def _L0_xattn_ref(query, key_value, Wq, Wk, Wv, Wo):
        import jax, jax.numpy as jnp
        import numpy as np
        D_MODEL = 128
        N_HEADS = 16
        HEAD_DIM = D_MODEL // N_HEADS
        B, S, _ = query.shape
        H, Dh = (N_HEADS, HEAD_DIM)
        q = (query @ Wq.T).reshape(B, S, H, Dh).transpose(0, 2, 1, 3)
        k = (key_value @ Wk.T).reshape(B, S, H, Dh).transpose(0, 2, 1, 3)
        v = (key_value @ Wv.T).reshape(B, S, H, Dh).transpose(0, 2, 1, 3)
        scale = Dh ** (-0.5)
        scores = jnp.einsum('bhqd,bhkd->bhqk', q, k) * scale
        causal = jnp.tril(jnp.ones((S, S), dtype=bool))
        scores = jnp.where(causal, scores, -jnp.inf)
        attn = jax.nn.softmax(scores, axis=-1)
        out = jnp.einsum('bhqk,bhkd->bhqd', attn, v)
        out = out.transpose(0, 2, 1, 3).reshape(B, S, H * Dh)
        return out @ Wo.T

    def _L0_ffn_ref(hidden_states, Wr, router_bias, Wg, Wu, Wd, conv_w, conv_b):
        import jax, jax.numpy as jnp
        import numpy as np
        from jax import lax
        H = 128
        E = 8
        E_MLP = E - 4
        TOP_K = 2
        I = 64
        KC = 4
        SHARED_SCALE = 1.0
        B, S, Hd = hidden_states.shape
        T = B * S
        x = hidden_states.reshape(T, Hd)
        scores = jax.nn.sigmoid(x @ Wr)
        _, idx = lax.top_k(scores + router_bias, TOP_K)
        w = jnp.take_along_axis(scores, idx, axis=-1)
        w = w / (jnp.sum(w, axis=-1, keepdims=True) + 1e-09)
        cw = jnp.zeros((T, E), dtype=x.dtype).at[jnp.arange(T)[:, None], idx].add(w)
        g = jnp.einsum('th,ehi->tei', x, Wg)
        u = jnp.einsum('th,ehi->tei', x, Wu)
        hid = jax.nn.silu(g) * u
        mlp_out = jnp.einsum('tei,eih->teh', hid, Wd)
        routed = jnp.einsum('te,teh->th', cw[:, :E_MLP], mlp_out)
        routed = routed + cw[:, E_MLP:E_MLP + 1] * x
        routed = routed + cw[:, E_MLP + 2:E_MLP + 3] * x
        routed = routed + cw[:, E_MLP + 3:E_MLP + 4] * jax.nn.relu(x)
        routed = routed.reshape(B, S, Hd)
        shared = lax.conv_general_dilated(hidden_states, conv_w, window_strides=(1,), padding=[(KC - 1, 0)], dimension_numbers=('NHC', 'HIO', 'NHC'), feature_group_count=Hd) + conv_b
        return routed + SHARED_SCALE * shared
    x = x + _L0_attn_ref(_layernorm(x, axis=-1), L0_attn_Wqkv, L0_attn_Wproj, L0_attn_bproj)
    x = x + _L0_xattn_ref(_layernorm(x, axis=-1), ctx_1024, L0_xattn_Wq, L0_xattn_Wk, L0_xattn_Wv, L0_xattn_Wo)
    x = x + _L0_ffn_ref(_layernorm(x, axis=-1), L0_ffn_Wr, L0_ffn_router_bias, L0_ffn_Wg, L0_ffn_Wu, L0_ffn_Wd, L0_ffn_conv_w, L0_ffn_conv_b)
    return x

_drawn_inputs = setup_inputs


def setup_inputs(seed=0):
    import zlib

    import numpy as np

    out = dict(_drawn_inputs(seed))
    spreads = {'L0_attn_bproj': (0.0, 0.1), 'L0_ffn_router_bias': (0.0, 0.1), 'L0_ffn_conv_b': (0.0, 0.1)}
    factors = {}
    for name, (base, spread) in spreads.items():
        noise = np.random.default_rng([zlib.crc32(name.encode()), seed]).standard_normal(out[name].shape)
        drawn = base * np.exp(spread * noise) if base else spread * noise
        out[name] = jnp.asarray(drawn.astype(out[name].dtype))
    for name, factor in factors.items():
        out[name] = (out[name] * factor).astype(out[name].dtype)
    return out
```

```python
import numpy as np
import concourse.bass as bass
from concourse import mybir
from contextlib import ExitStack

B, S, C, H, D = 8, 256, 128, 16, 8
E, EM, I = 8, 4, 64
KC = 4
P = 128
T = S // P
HALF = H // 2
TERM_ROWS = 6 * D
MAX_ROW = 64
STACK = 96
EXP_UNITS = 12
MAX_UNITS = 14
VW = 32

WEIGHTS = [("qkv", 3 * C), ("proj", C), ("q", C), ("k", C), ("v", C), ("o", C), ("gate", EM * I),
           ("up", EM * I), ("down", 2 * C), ("router", E), ("conv", KC), ("conv_b", 1)]

SLOTS = [
    [("load", 3, 0), ("soft", 0, 0), ("max", 1, 4), ("norm2", 2, 0)],
    [("soft", 0, 1), ("max", 1, 5), ("pv", -1, 3), ("self_norm_t", 2, 0)],
    [("soft", 0, 2), ("maxrow", 1, 0), ("max", 1, 6), ("self_q2", 2, 0)],
    [("soft", 0, 3), ("max", 1, 7), ("self_k", 2, 0), ("ffn_out_t", -1, 0), ("norm1", 3, 0)],
    [("soft", 0, 4), ("max", 1, 8), ("pv", 0, 0), ("self_v", 1, 0), ("ffn_o2_t", -1, 0), ("clear", 3, 0)],
    [("soft", 0, 5), ("max", 1, 9), ("self_x_t", 3, 0), ("ffn_o", -1, 0), ("norm3", -1, 0)],
    [("soft", 0, 6), ("stack", 2, 0), ("max", 1, 10), ("self_q1", 3, 0)],
    [("soft", 0, 7), ("max", 1, 11), ("pv", 0, 1), ("self_kv", 3, 0), ("ffn_x_t", -1, 0), ("park", 1, 0)],
    [("soft", 0, 8), ("maxrow", 1, 1), ("max", 2, 0), ("self_sum", 3, 0), ("ffn_router", -1, 0), ("ffn_gate", -1, 0)],
    [("soft", 0, 9), ("max", 2, 1), ("self_out", 3, 0), ("ffn_up", -1, 0)],
    [("soft", 0, 10), ("max", 2, 2), ("pv", 0, 2), ("self_o_t", 3, 0), ("ffn_cw", -1, 0)],
    [("soft", 0, 11), ("stack", 2, 1), ("max", 2, 3), ("self_proj", 3, 0), ("ffn_down", -1, 0)],
]
FIRST_ROUND, LAST_ROUND = -3, B
LOOP_FROM, LOOP_TRIPS = 1, 2


class Batch:

    def __init__(self, trip, c):
        self.trip, self.c = trip, c
        self.par = c % 2

    def count(self, per, plus=0):
        assert per * self.c + plus >= (0 if isinstance(self.trip, int) else 1)
        return self.trip * (2 * per) + (per * self.c + plus)

    def pair(self, per, plus=0):
        assert per * (self.c // 2) + plus >= 0
        return self.trip * per + (per * (self.c // 2) + plus)

    def since(self, n):
        assert isinstance(self.trip, int) or self.c >= n
        return self.c >= n

    @property
    def number(self):
        return self.trip * 2 + self.c if self.c else self.trip * 2


def rounds(engine, steps):
    def one(trip, r):
        for slot in SLOTS:
            for name, off, arg in slot:
                in_loop = LOOP_FROM <= r < LOOP_FROM + 2 * LOOP_TRIPS
                if name in steps and (in_loop or 0 <= r + off < B):
                    steps[name](Batch(trip, r + off), arg)

    r = FIRST_ROUND
    while r <= LAST_ROUND:
        if r == LOOP_FROM:
            with engine.Fori(0, LOOP_TRIPS) as trip:
                one(trip, r)
                one(trip, r + 1)
            r += 2 * LOOP_TRIPS
        else:
            one(0, r)
            r += 1


def build(nc, x, ctxT, weights, bproj, router_bias, out):
    f32, bf16 = mybir.dt.float32, mybir.dt.bfloat16
    ALU, ACT, AX = mybir.AluOpType, mybir.ActivationFunctionType, mybir.AxisListType
    scale = float(D) ** -0.5

    ctx = ExitStack()
    with ctx:
        def sb(name, shape, dt=f32):
            return ctx.enter_context(nc.sbuf_tensor(name, shape, dt))

        def pb(name):
            return ctx.enter_context(nc.psum_tensor(name, [P, 512], f32))

        def sem(name):
            return ctx.enter_context(nc.semaphore(name))

        ctx.enter_context(nc.allow_non_contiguous_dma(reason="rows of 512 bytes"))
        ctx.enter_context(nc.allow_low_precision(reason="exact splits into bfloat16 parts"))

        parts_dram = {n: nc.dram_tensor(f"{n}_parts", [2, 2, 3, D, HALF, S], bf16, kind="Internal").ap()
                      for n in "qk"}

        W = sb("W", [P, sum(n for _, n in WEIGHTS)])
        w, at = {}, 0
        for name, n in WEIGHTS:
            w[name] = W[:, at:at + n]
            at += n
        bproj_all = sb("bproj_all", [P, C])
        rbias_all = sb("rbias_all", [P, E])
        ident = sb("ident", [P, P])
        identb = sb("identb", [P, P], bf16)
        causal = sb("causal", [P, 512], bf16)
        headmask = sb("headmask", [P, C])
        headsel = sb("headsel", [P, H])
        exponent = sb("exponent", [P, T])
        first_rank = sb("first_rank", [P, T * E])
        zero_rows = sb("zero_rows", [2, HALF * S], bf16)

        xin = [sb(f"xin{i}", [P, T, C]) for i in range(2)]
        ctxin = [sb(f"ctxin{i}", [C, S]) for i in range(2)]
        norm = {}
        for n in (1, 2, 3):
            norm[n] = dict(stats=sb(f"stats{n}", [P, T, 6]), mv=sb(f"mv{n}", [P, T, 2]),
                           vareps=sb(f"vareps{n}", [P, T]), negmean=sb(f"negmean{n}", [P, T]),
                           rstd=sb(f"rstd{n}", [P, T]), shift=sb(f"shift{n}", [P, T]),
                           out=sb(f"xn{n}", [P, T, C]))
        xnT = sb("xnT", [C, S])
        expq, reluq, phiq = sb("expq", [C, S]), sb("reluq", [C, S]), sb("phiq", [C, S])
        expk, reluk, phik = sb("expk", [P, T, C]), sb("reluk", [P, T, C]), sb("phik", [P, T, C])
        vones = sb("vones", [P, T, C + 1])
        kvsum = sb("kvsum", [C, C + H])
        den1, rden1 = sb("den1", [P, T, H]), sb("rden1", [P, T, H])
        o1, o1T = sb("o1", [P, T, C]), sb("o1T", [C, S])
        xres = sb("xres", [P, T, C])
        x1 = [sb(f"x1_{i}", [P, T, C]) for i in range(2)]
        x1_parked = [sb(f"x1_parked{i}", [P, T, C]) for i in range(2)]
        x2nT = sb("x2nT", [C, S])
        parts = {n: sb(f"{n}parts", [C, 3, S], bf16) for n in "qk"}
        rest = {n: sb(f"{n}rest", [C, S]) for n in "qk"}
        qs = [sb(f"qs{i}", [STACK, H, S], bf16) for i in range(2)]
        ks = [sb(f"ks{i}", [STACK, H, S], bf16) for i in range(2)]
        vs = [sb(f"vs{i}", [P, T, H, VW]) for i in range(2)]
        negmax = sb("negmax", [P, 2, HALF, T])
        maxparts = [sb(f"maxparts{i}", [T * HALF, 2, P], bf16) for i in range(2)]
        probs = [sb(f"probs{i}", [P, 3, 512]) for i in range(2)]
        outT = sb("outT", [P, 4, S])
        rden2 = [sb(f"rden2_{i}", [P, H]) for i in range(2)]
        o2, o2T = sb("o2", [P, T, C]), sb("o2T", [C, S])
        x2 = sb("x2", [P, T, C])
        x3T = sb("x3T", [C, KC - 1 + S])
        tanr, sig, biased = sb("tanr", [P, T * E]), sb("sig", [P, T * E]), sb("biased", [P, T * E])
        top = sb("top", [P, T])
        is_top, rank, pick1, pick2 = (sb(n, [P, T * E]) for n in ("is_top", "rank", "pick1", "pick2"))
        wsel, wsum, cw = sb("wsel", [P, T * E]), sb("wsum", [P, T]), sb("cw", [P, T * E])
        cskip = sb("cskip", [P, T])
        cw_wide = sb("cw_wide", [P, T, EM * I])
        tang, gated, hid0, hid, cwT = (sb(n, [P, 2 * S]) for n in ("tang", "gated", "hid0", "hid", "cwT"))
        conv, tap = sb("conv", [C, S]), sb("tap", [C, S])
        relu7, skip, base = sb("relu7", [P, T, C]), sb("skip", [P, T, C]), sb("base", [P, T, C])
        result = sb("result", [P, T, C])

        soft_bank = [pb(f"soft_bank{i}") for i in range(2)]
        max_bank = [pb(f"max_bank{i}") for i in range(2)]
        pv_bank, self_bank = pb("pv_bank"), pb("self_bank")
        ffn_bank = [pb(f"ffn_bank{i}") for i in range(2)]

        weights_in, bias_in, consts, cleared = sem("weights_in"), sem("bias_in"), sem("consts"), sem("cleared")
        x_in = [sem(f"x_in{i}") for i in range(2)]
        ctx_in = [sem(f"ctx_in{i}") for i in range(2)]
        stats_done = {n: sem(f"stats_done{n}") for n in norm}
        mv_done = {n: sem(f"mv_done{n}") for n in norm}
        rstd_done = {n: sem(f"rstd_done{n}") for n in norm}
        xn_done = {n: sem(f"xn_done{n}") for n in norm}
        pe_x_t, pe_q1, pe_kv, pe_sum, pe_out1, pe_o_t, pe_proj = (
            sem(n) for n in ("pe_x_t", "pe_q1", "pe_kv", "pe_sum", "pe_out1", "pe_o_t", "pe_proj"))
        pe_norm_t, pe_q2, pe_k, pe_v = (sem(n) for n in ("pe_norm_t", "pe_q2", "pe_k", "pe_v"))
        xnT_done, q_act, k_act = sem("xnT_done"), sem("q_act"), sem("k_act")
        phiq_done, phik_done, kvsum_done = sem("phiq_done"), sem("phik_done"), sem("kvsum_done")
        o1_steps, o1T_done, xres_done, x1_done = (
            sem(n) for n in ("o1_steps", "o1T_done", "xres_done", "x1_done"))
        x2nT_done = sem("x2nT_done")
        hi_done, mid_done, rest_done, rest2_done, lo_done = (
            {n: sem(f"{n}_{s}") for n in "qk"} for s in ("hi_done", "mid_done", "rest_done", "rest2_done", "lo_done"))
        stored = {n: sem(f"{n}_stored") for n in "qk"}
        stack_in = [sem(f"stack_in{i}") for i in range(2)]
        max_in = [sem(f"max_in{i}") for i in range(2)]
        vs_done, parked = sem("vs_done"), [sem(f"parked{i}") for i in range(2)]
        pe_soft, exp_done, masked = sem("pe_soft"), sem("exp_done"), sem("masked")
        pe_max, max_read = sem("pe_max"), sem("max_read")
        pe_maxrow, maxhi_done = sem("pe_maxrow"), sem("maxhi_done")
        pe_pv, outT_done = sem("pe_pv"), sem("outT_done")
        pe_out_t, o2_steps = sem("pe_out_t"), sem("o2_steps")
        pe_o2_t, o2T_done, pe_o, x2_done, pe_ffn_x_t, x3T_done = (
            sem(n) for n in ("pe_o2_t", "o2T_done", "pe_o", "x2_done", "pe_ffn_x_t", "x3T_done"))
        pe_router, tanr_done, route = sem("pe_router"), sem("tanr_done"), sem("route")
        pe_gate, tang_done, gated_done, pe_up, hid0_done, pe_cw, cwT_done, hid_done, pe_down = (
            sem(n) for n in ("pe_gate", "tang_done", "gated_done", "pe_up", "hid0_done", "pe_cw",
                             "cwT_done", "hid_done", "pe_down"))
        conv_steps, relu7_done, skip_done, base_done, result_done, out_stored = (
            sem(n) for n in ("conv_steps", "relu7_done", "skip_done", "base_done", "result_done", "out_stored"))
        cskip_done, cw_wide_done = sem("cskip_done"), sem("cw_wide_done")
        CONV = 2 * KC - 1
        ROUTE = 19
        N_CONSTS = 7 + 5 + 2 + E + 1
        N_CLEARED = 11
        K_LOADS, Q_LOADS = 3, 6
        STACK_IN = 16 * (K_LOADS + Q_LOADS + 1)

        block = ctx.enter_context(nc.Block())

        def settle(engine, *counts):
            for count in counts:
                if not isinstance(count, int):
                    engine.lower_val(count)
            engine.wait_ge(consts, 1)

        def group_view(bank, n):
            return bank[:, 0:512].rearrange("p (n c) -> p n c", n=n)

        @block.sync
        def _(sp):
            def load_x(b):
                sp.dma_start(xin[b.par][:, :, :], x_v[b.number]).then_inc(x_in[b.par], 16)

            def load_ctx(b):
                sp.dma_start(ctxin[b.par][:, :], ctx_v[b.number]).then_inc(ctx_in[b.par], 16)

            x_v = x.rearrange("b (t p) c -> b p t c", p=P)
            out_v = out.rearrange("b (t p) c -> b p t c", p=P)
            ctx_v = ctxT.rearrange("c (b s) -> b c s", s=S)

            load_x(Batch(0, 0))
            sp.dma_start(W[:, :], weights).then_inc(weights_in, 16)
            sp.dma_start(bproj_all[:, :], bproj.unsqueeze(0).to_broadcast([P, C])).then_inc(bias_in, 16)
            sp.dma_start(rbias_all[:, :], router_bias.unsqueeze(0).to_broadcast([P, E])).then_inc(bias_in, 16)
            load_ctx(Batch(0, 0))
            load_x(Batch(0, 1))
            load_ctx(Batch(0, 1))

            def load(b, _):
                if b.since(2):
                    reached = b.count(1, -1)
                    settle(sp, reached)
                    sp.wait_ge(x1_done, reached)
                    load_x(b)

            def load_context(b, _):
                if b.since(2):
                    reached = b.count(1, -1)
                    settle(sp, reached)
                    sp.wait_ge(vs_done, reached)
                    load_ctx(b)

            def store_parts(n):
                def go(b, _):
                    lo = b.count(1, 1)
                    if b.since(2):
                        read = b.count(STACK_IN, -STACK_IN)
                        for half in range(2):
                            sp.wait_ge(stack_in[half], read)
                    sp.wait_ge(lo_done[n], lo)
                    for half in range(2):
                        sp.dma_start(parts_dram[n][b.par, half].rearrange("part d h s -> (d h) part s"),
                                     parts[n][64 * half:64 * half + 64, :, :]).then_inc(stored[n], 16)
                return go

            def stack(b, half):
                all_stored = b.count(32, 32)
                softened = b.count(EXP_UNITS, -2 * EXP_UNITS + 6 * (half + 1)) if b.since(2) else None
                settle(sp, all_stored, softened if b.since(2) else 0)
                sp.wait_ge(cleared, N_CLEARED)
                sp.wait_ge(stored["q"], all_stored)
                sp.wait_ge(stored["k"], all_stored)
                if b.since(2):
                    sp.wait_ge(pe_soft, softened)
                rows = {n: parts_dram[n][b.par, half].rearrange("part d h s -> (part d) (h s)") for n in "qk"}
                heads = slice(HALF * half, HALF * half + HALF)
                at = 0
                for n_rows in (3 * D, 2 * D, D):
                    sp.dma_start(ks[b.par][at:at + n_rows, heads, :].rearrange("r h s -> r (h s)"),
                                 rows["k"][0:n_rows, :]).then_inc(stack_in[half], 16)
                    at += n_rows
                at = 0
                for part in (0, 0, 0, 1, 1, 2):
                    sp.dma_start(qs[b.par][at:at + D, heads, :].rearrange("r h s -> r (h s)"),
                                 rows["q"][D * part:D * part + D, :]).then_inc(stack_in[half], 16)
                    at += D
                sp.dma_start(qs[b.par][MAX_ROW:MAX_ROW + 2, heads, :].rearrange("r h s -> r (h s)"),
                             zero_rows[:, :]).then_inc(stack_in[half], 16)

            def store_maxrow(b, half):
                sp.wait_ge(max_read, b.count(MAX_UNITS, 7 * (half + 1)))
                for part in range(2):
                    row = qs[b.par][MAX_ROW + part:MAX_ROW + part + 1, HALF * half:HALF * half + HALF, :]
                    sp.dma_start(row.rearrange("r h (t q) -> r (h t) q", t=T),
                                 maxparts[half][:, part, :]).then_inc(max_in[half], 16)

            def park(b, _):
                written = b.count(1, 1)
                if b.since(2):
                    sp.wait_ge(x2_done, b.count(1, -1))
                sp.wait_ge(x1_done, written)
                sp.dma_start(x1_parked[b.par][:, :, :], x1[b.par][:, :, :]).then_inc(parked[b.par], 16)

            def store_out(b, _):
                reached = b.count(1, 2)
                settle(sp, reached)
                sp.wait_ge(result_done, reached)
                sp.dma_start(out_v[b.number], result[:, :, :]).then_inc(out_stored, 16)

            rounds(sp, {"load": load, "self_q1": load_context, "self_q2": store_parts("q"), "self_k": store_parts("k"),
                        "stack": stack, "maxrow": store_maxrow, "park": park, "ffn_down": store_out})
            sp.wait_ge(out_stored, 16 * B + 1)


        @block.gpsimd
        def _(pool):
            def const(ins):
                ins.then_inc(consts, 1)

            nc.gpsimd.memset(result[:, :, :], 0.0).then_inc(result_done, 1)
            nc.gpsimd.memset(top[:, :], 0.0).then_inc(out_stored, 1)
            const(nc.gpsimd.memset(exponent[:, :], -0.5))
            const(nc.gpsimd.memset(ident[:, :], 0.0))
            const(nc.gpsimd.memset(headmask[:, :], 1.0))
            const(nc.gpsimd.memset(headsel[:, :], 1.0))
            const(nc.gpsimd.memset(vones[:, :, C:C + 1], 1.0))
            const(nc.gpsimd.memset(causal[:, :], 0.0))
            const(nc.gpsimd.memset(identb[:, :], 0.0))
            pool.wait_ge(consts, 7)
            const(nc.gpsimd.affine_select(out=identb[:, :], in_=identb[:, :], compare_op=ALU.not_equal, fill=1.0,
                                          base=0, pattern=[[-1, P]], channel_multiplier=1))
            const(nc.gpsimd.affine_select(out=group_view(causal, 4), in_=group_view(causal, 4), compare_op=ALU.is_ge,
                                          fill=-1e30, base=0, pattern=[[0, 4], [-1, P]], channel_multiplier=1))
            const(nc.gpsimd.affine_select(out=ident[:, :], in_=ident[:, :], compare_op=ALU.not_equal, fill=1.0,
                                          base=0, pattern=[[-1, P]], channel_multiplier=1))
            for tile, pat in ((headmask[:, :].rearrange("p (h m) -> p h m", h=H), [[-D, H], [0, D]]),
                              (headsel[:, :], [[-D, H]])):
                const(nc.gpsimd.affine_select(out=tile, in_=tile, compare_op=ALU.is_ge, fill=0.0,
                                              base=0, pattern=pat, channel_multiplier=1))
            pool.wait_ge(consts, 12)
            for tile, pat in ((headmask[:, :].rearrange("p (h m) -> p h m", h=H), [[D, H], [0, D]]),
                              (headsel[:, :], [[D, H]])):
                const(nc.gpsimd.affine_select(out=tile, in_=tile, compare_op=ALU.is_ge, fill=0.0,
                                              base=D - 1, pattern=pat, channel_multiplier=-1))
            for e in range(E):
                const(nc.gpsimd.memset(first_rank[:, :].rearrange("p (t e) -> p t e", t=T)[:, :, e], float(E - e)))
            const(nc.gpsimd.memset(x3T[:, 0:KC - 1], 0.0))

            def rstd(n):
                t = norm[n]

                def go(b, _):
                    before = n != 3 and b.since(1)
                    ready, free = b.count(2, 2), b.count(2) if before else 0
                    settle(pool, ready, free)
                    pool.wait_ge(mv_done[n], ready)
                    if before:
                        pool.wait_ge(xn_done[n], free)
                    nc.gpsimd.tensor_scalar(t["vareps"][:, :], t["mv"][:, :, 1], 1e-5, None, ALU.add).then_inc(rstd_done[n], 1)
                    nc.gpsimd.tensor_scalar(t["negmean"][:, :], t["mv"][:, :, 0], -1.0, 1.0, ALU.mult, ALU.mult).then_inc(rstd_done[n], 1)
                    pool.wait_ge(rstd_done[n], b.count(4, 1))
                    nc.gpsimd.tensor_tensor(t["rstd"][:, :], t["vareps"][:, :], exponent[:, :], ALU.pow).then_inc(rstd_done[n], 1)
                    pool.wait_ge(rstd_done[n], b.count(4, 3))
                    nc.gpsimd.tensor_tensor(t["shift"][:, :], t["negmean"][:, :], t["rstd"][:, :], ALU.mult).then_inc(rstd_done[n], 1)
                return go

            def add_bias(b, _):
                pool.wait_ge(x_in[b.par], b.pair(16, 16))
                pool.wait_ge(bias_in, 32)
                if b.since(1):
                    pool.wait_ge(x1_done, b.count(1))
                nc.gpsimd.tensor_tensor(xres[:, :, :], xin[b.par][:, :, :],
                                        bproj_all[:, :].unsqueeze(1).to_broadcast([P, T, C]), ALU.add).then_inc(xres_done, 1)

            def lowest_part(n):
                def go(b, _):
                    pool.wait_ge(mid_done[n], b.count(1, 1))
                    if b.since(1):
                        pool.wait_ge(stored[n], b.count(32))
                    nc.gpsimd.tensor_tensor(parts[n][:, 2, :], rest[n][:, :], parts[n][:, 1, :], ALU.subtract).then_inc(lo_done[n], 1)
                return go

            def mask_probs(b, u):
                g, k = divmod(u, 3)
                ready = b.count(EXP_UNITS, u + 1)
                settle(pool, ready)
                pool.wait_ge(exp_done, ready)
                n = 4 if k == 2 else 2
                v = probs[g % 2][:, k, :].rearrange("p (n q) -> p n q", n=n)[:, :, 0:P]
                nc.gpsimd.affine_select(out=v, in_=v, compare_op=ALU.is_ge, fill=0.0, base=0,
                                        pattern=[[0, n], [1, P]], channel_multiplier=-1).then_inc(masked, 1)

            def convolve(b, _):
                ready = b.count(1, 1)
                settle(pool, ready)
                pool.wait_ge(x3T_done, ready)
                pool.wait_ge(weights_in, 16)
                nc.gpsimd.tensor_scalar(conv[:, :], x3T[:, KC - 1:KC - 1 + S], w["conv"][:, KC - 1:KC], w["conv_b"],
                                        ALU.mult, ALU.add).then_inc(conv_steps, 1)
                for j in range(KC - 1):
                    added = b.count(CONV, 2 * j + 1)
                    settle(pool, added)
                    pool.wait_ge(conv_steps, added)
                    nc.gpsimd.tensor_scalar(tap[:, :], x3T[:, j:j + S], w["conv"][:, j:j + 1], 1.0,
                                            ALU.mult, ALU.mult).then_inc(conv_steps, 1)
                    pool.wait_ge(conv_steps, b.count(CONV, 2 * j + 2))
                    nc.gpsimd.tensor_tensor(conv[:, :], conv[:, :], tap[:, :], ALU.add).then_inc(conv_steps, 1)

            def weigh_hidden(b, _):
                pool.wait_ge(hid0_done, b.count(1, 1))
                pool.wait_ge(cwT_done, b.count(1, 1))
                nc.gpsimd.tensor_tensor(hid[:, :], hid0[:, :], cwT[:, :], ALU.mult).then_inc(hid_done, 1)
                pool.wait_ge(relu7_done, b.count(2, 2))
                pool.wait_ge(skip_done, b.count(2, 2))
                nc.gpsimd.tensor_tensor(base[:, :, :], skip[:, :, :], relu7[:, :, :], ALU.add).then_inc(base_done, 1)

            rounds(pool, {"norm1": rstd(1), "norm2": rstd(2), "norm3": rstd(3), "self_sum": add_bias,
                          "self_q2": lowest_part("q"), "self_k": lowest_part("k"), "soft": mask_probs,
                          "ffn_router": convolve, "ffn_cw": weigh_hidden})

        @block.scalar
        def _(act):
            def normalise(n):
                t = norm[n]

                def go(b, _):
                    act.wait_ge(rstd_done[n], b.count(4, 4))
                    source = {1: xin[b.par], 2: x1[b.par], 3: x2}[n]
                    if n == 1:
                        act.wait_ge(x_in[b.par], b.pair(16, 16))
                    if n != 3 and b.since(1):
                        act.wait_ge({1: pe_x_t, 2: pe_norm_t}[n], b.count(1))
                    for i in range(T):
                        nc.scalar.activation(t["out"][:, i, :], source[:, i, :], ACT.Identity,
                                             scale=t["rstd"][:, i:i + 1], bias=t["shift"][:, i:i + 1]).then_inc(xn_done[n], 1)
                return go

            def copy_xnT(b, _):
                act.wait_ge(pe_x_t, b.count(1, 1))
                if b.since(1):
                    act.wait_ge(pe_kv, b.count(1))
                nc.scalar.copy(xnT[:, :], self_bank[:, 0:S]).then_inc(xnT_done, 1)

            def act_q(b, _):
                act.wait_ge(pe_q1, b.count(1, 1))
                if b.since(1):
                    act.wait_ge(phiq_done, b.count(1))
                nc.scalar.activation(expq[:, :], self_bank[:, 0:S], ACT.Exp).then_inc(q_act, 1)
                nc.scalar.activation(reluq[:, :], self_bank[:, 0:S], ACT.Relu).then_inc(q_act, 1)

            def act_kv(b, _):
                act.wait_ge(pe_kv, b.count(1, 1))
                if b.since(1):
                    act.wait_ge(phik_done, b.count(1))
                    act.wait_ge(pe_sum, b.count(1))
                kv = group_view(self_bank, T)
                nc.scalar.activation(expk[:, :, :], kv[:, :, 0:C], ACT.Exp).then_inc(k_act, 1)
                nc.scalar.activation(reluk[:, :, :], kv[:, :, 0:C], ACT.Relu).then_inc(k_act, 1)
                nc.scalar.copy(vones[:, :, 0:C], kv[:, :, C:2 * C]).then_inc(k_act, 1)

            def copy_o1T(b, _):
                act.wait_ge(pe_o_t, b.count(1, 1))
                if b.since(1):
                    act.wait_ge(pe_proj, b.count(1))
                nc.scalar.copy(o1T[:, :], self_bank[:, 0:S]).then_inc(o1T_done, 1)

            def copy_x2nT(b, _):
                act.wait_ge(pe_norm_t, b.count(1, 1))
                if b.since(1):
                    act.wait_ge(pe_q2, b.count(1))
                nc.scalar.copy(x2nT[:, :], self_bank[:, 0:S]).then_inc(x2nT_done, 1)

            def high_parts(n, pe_done, factor):
                def go(b, _):
                    act.wait_ge(pe_done, b.count(1, 1))
                    if b.since(1):
                        act.wait_ge(stored[n], b.count(32))
                    nc.scalar.mul(parts[n][:, 0, :], self_bank[:, 0:S], factor).then_inc(hi_done[n], 1)
                    act.wait_ge(rest_done[n], b.count(1, 1))
                    nc.scalar.copy(parts[n][:, 1, :], rest[n][:, :]).then_inc(mid_done[n], 1)
                return go

            def copy_v(b, _):
                act.wait_ge(pe_v, b.count(1, 1))
                act.wait_ge(cleared, N_CLEARED)
                if b.since(2):
                    act.wait_ge(pe_pv, b.count(4, -4))
                nc.scalar.copy(vs[b.par][:, :, :, 0:D], self_bank[:, 0:S].rearrange("p (t h d) -> p t h d", t=T, h=H)).then_inc(vs_done, 1)

            def exp_scores(b, u):
                g, k = divmod(u, 3)
                act.wait_ge(pe_soft, b.count(EXP_UNITS, u + 1))
                if g >= 2 or b.since(1):
                    act.wait_ge(pe_pv, b.count(4, g - 1))
                nc.scalar.activation(probs[g % 2][:, k, :], soft_bank[u % 2][:, :], ACT.Exp).then_inc(exp_done, 1)

            def max_high(b, half):
                act.wait_ge(pe_maxrow, b.count(2, half + 1))
                if b.since(1):
                    act.wait_ge(max_in[half], b.count(32))
                k = 6 if half == 0 else 13
                nc.scalar.copy(maxparts[half][:, 0, :], max_bank[k % 2][0:T * HALF, 0:P]).then_inc(maxhi_done, 1)

            def copy_outT(b, g):
                act.wait_ge(pe_pv, b.count(4, g + 1))
                if g == 0 and b.since(1):
                    act.wait_ge(pe_out_t, b.count(2))
                nc.scalar.copy(outT[:, g, :], pv_bank[:, 0:S]).then_inc(outT_done, 1)

            def copy_o2T(b, _):
                act.wait_ge(pe_o2_t, b.count(1, 1))
                nc.scalar.copy(o2T[:, :], ffn_bank[0][:, 0:S]).then_inc(o2T_done, 1)

            def copy_x3T(b, _):
                act.wait_ge(pe_ffn_x_t, b.count(1, 1))
                nc.scalar.copy(x3T[:, KC - 1:KC - 1 + S], ffn_bank[0][:, 0:S]).then_inc(x3T_done, 1)

            def tanh_router(b, _):
                act.wait_ge(pe_router, b.count(1, 1))
                nc.scalar.activation(tanr[:, :], ffn_bank[1][:, 0:T * E], ACT.Tanh, scale=0.5).then_inc(tanr_done, 1)

            def tanh_gate(b, _):
                act.wait_ge(pe_gate, b.count(1, 1))
                nc.scalar.activation(tang[:, :], ffn_bank[0][:, :], ACT.Tanh, scale=0.5).then_inc(tang_done, 1)

            def copy_cw(b, _):
                act.wait_ge(route, b.count(ROUTE, ROUTE))
                for i in range(T):
                    nc.scalar.activation(relu7[:, i, :], norm[3]["out"][:, i, :], ACT.Relu,
                                         scale=cw[:, i * E + 7:i * E + 8]).then_inc(relu7_done, 1)
                nc.scalar.activation(cw_wide[:, :, :].rearrange("p t (e i) -> p t e i", e=EM),
                                     cw[:, :].rearrange("p (t e) -> p t e", t=T)[:, :, 0:EM].unsqueeze(3).to_broadcast([P, T, EM, I]),
                                     ACT.Copy, scale=0.5).then_inc(cw_wide_done, 1)
                act.wait_ge(pe_cw, b.count(1, 1))
                nc.scalar.copy(cwT[:, :], ffn_bank[0][:, :]).then_inc(cwT_done, 1)

            rounds(act, {"norm1": normalise(1), "norm2": normalise(2), "norm3": normalise(3), "self_x_t": copy_xnT,
                         "self_q1": act_q, "self_kv": act_kv, "self_o_t": copy_o1T, "self_norm_t": copy_x2nT,
                         "self_q2": high_parts("q", pe_q2, scale), "self_k": high_parts("k", pe_k, 1.0), "self_v": copy_v,
                         "soft": exp_scores, "maxrow": max_high, "pv": copy_outT, "ffn_o2_t": copy_o2T,
                         "ffn_x_t": copy_x3T, "ffn_router": tanh_router, "ffn_gate": tanh_gate, "ffn_cw": copy_cw})

        @block.vector
        def _(dve):
            def clear_stacks(b, _):
                if b.since(1):
                    return
                for tile in qs + ks:
                    nc.vector.memset(tile[:, :, :].rearrange("r h s -> r (h s)").bitcast(f32), 0.0).then_inc(cleared, 1)
                for tile in vs:
                    nc.vector.memset(tile[:, :, :, :], 0.0).then_inc(cleared, 1)
                nc.vector.memset(zero_rows[:, :].bitcast(f32), 0.0).then_inc(cleared, 1)
                dve.wait_ge(cleared, 7)
                for tile in ks:
                    nc.vector.memset(tile[MAX_ROW:MAX_ROW + 2, :, :], 1.0).then_inc(cleared, 1)
                for tile in vs:
                    nc.vector.memset(tile[:, :, :, D], 1.0).then_inc(cleared, 1)

            def stats(n):
                t = norm[n]

                def go(b, _):
                    source = {1: xin[b.par], 2: x1[b.par], 3: x2}[n]
                    if n == 1:
                        dve.wait_ge(x_in[b.par], b.pair(16, 16))
                    else:
                        dve.wait_ge({2: x1_done, 3: x2_done}[n], b.count(1, 1))
                    if n != 3 and b.since(1):
                        dve.wait_ge(rstd_done[n], b.count(4))
                    for i in range(T):
                        nc.vector.bn_stats(t["stats"][:, i, :], source[:, i, :]).then_inc(stats_done[n], 1)
                    ready = b.count(2, 2)
                    settle(dve, ready)
                    dve.wait_ge(stats_done[n], ready)
                    for i in range(T):
                        nc.vector.bn_aggr(t["mv"][:, i, :], t["stats"][:, i, :]).then_inc(mv_done[n], 1)
                return go

            def phi_q(b, _):
                dve.wait_ge(q_act, b.count(2, 2))
                if b.since(1):
                    dve.wait_ge(pe_out1, b.count(1))
                nc.vector.scalar_tensor_tensor(out=phiq[:, :], in0=expq[:, :], scalar=1.0, in1=reluq[:, :],
                                               op0=ALU.min, op1=ALU.add).then_inc(phiq_done, 1)

            def phi_k(b, _):
                dve.wait_ge(k_act, b.count(3, 2))
                if b.since(1):
                    dve.wait_ge(pe_sum, b.count(1))
                nc.vector.scalar_tensor_tensor(out=phik[:, :, :], in0=expk[:, :, :], scalar=1.0, in1=reluk[:, :, :],
                                               op0=ALU.min, op1=ALU.add).then_inc(phik_done, 1)

            def mask_kvsum(b, _):
                dve.wait_ge(pe_sum, b.count(1, 1))
                dve.wait_ge(consts, N_CONSTS)
                if b.since(1):
                    dve.wait_ge(pe_out1, b.count(1))
                nc.vector.tensor_tensor(kvsum[:, 0:C], self_bank[:, 0:C], headmask[:, :], ALU.mult).then_inc(kvsum_done, 1)
                nc.vector.tensor_scalar(kvsum[:, C:C + H], headsel[:, :], self_bank[:, C:C + 1], None, ALU.mult).then_inc(kvsum_done, 1)

            def divide_out1(b, _):
                dve.wait_ge(pe_out1, b.count(1, 1))
                if b.since(1):
                    dve.wait_ge(pe_o_t, b.count(1))
                both = self_bank[:, 0:T * (C + H)].rearrange("p (t c) -> p t c", t=T)
                nc.vector.tensor_scalar(den1[:, :, :], both[:, :, C:C + H], 1e-6, None, ALU.add).then_inc(o1_steps, 1)
                dve.wait_ge(o1_steps, b.count(3, 1))
                nc.vector.reciprocal(rden1[:, :, :], den1[:, :, :]).then_inc(o1_steps, 1)
                dve.wait_ge(o1_steps, b.count(3, 2))
                for i in range(T):
                    ins = nc.vector.tensor_tensor(o1[:, i, :].rearrange("p (h m) -> p h m", h=H),
                                                  both[:, i, 0:C].rearrange("p (h m) -> p h m", h=H),
                                                  rden1[:, i, :].unsqueeze(2).to_broadcast([P, H, D]), ALU.mult)
                ins.then_inc(o1_steps, 1)

            def residual1(b, _):
                dve.wait_ge(pe_proj, b.count(1, 1))
                dve.wait_ge(xres_done, b.count(1, 1))
                if b.since(2):
                    dve.wait_ge(parked[b.par], b.pair(16))
                    dve.wait_ge(xn_done[2], b.count(2, -2))
                nc.vector.tensor_tensor(x1[b.par][:, :, :], self_bank[:, 0:S].rearrange("p (t c) -> p t c", t=T),
                                        xres[:, :, :], ALU.add).then_inc(x1_done, 1)

            def remainder(n, factor):
                def go(b, _):
                    dve.wait_ge(hi_done[n], b.count(1, 1))
                    if b.since(1):
                        dve.wait_ge(lo_done[n], b.count(1))
                    nc.vector.scalar_tensor_tensor(out=rest[n][:, :], in0=self_bank[:, 0:S], scalar=factor,
                                                   in1=parts[n][:, 0, :], op0=ALU.mult, op1=ALU.subtract).then_inc(rest_done[n], 1)
                return go

            def reduce_scores(b, u):
                g, k = divmod(u, 3)
                half = g // 2
                dve.wait_ge(pe_max, b.count(EXP_UNITS, u + 1))
                if b.since(1):
                    dve.wait_ge(pe_maxrow, b.count(2, half - 1))
                at, n = (4 * (g % 2), 4) if k == 0 else (4 * (g % 2) + 2 * (k - 1), 2)
                nc.vector.tensor_reduce(negmax[:, half, at:at + n, min(k, 1)], group_view(max_bank[(u + half) % 2], n),
                                        AX.X, ALU.max, negate=True).then_inc(max_read, 1)

            def max_mid(b, half):
                dve.wait_ge(maxhi_done, b.count(2, half + 1))
                if b.since(1):
                    dve.wait_ge(max_in[half], b.count(32))
                k = 6 if half == 0 else 13
                nc.vector.tensor_tensor(maxparts[half][:, 1, :], max_bank[k % 2][0:T * HALF, 0:P],
                                        maxparts[half][:, 0, :], ALU.subtract).then_inc(max_read, 1)

            def divide_out2(b, _):
                for i in range(T):
                    dve.wait_ge(pe_out_t, b.count(2, i + 1))
                    heads = ffn_bank[i][:, :].rearrange("p (h m) -> p h m", h=H)
                    nc.vector.reciprocal(rden2[i][:, :], heads[:, :, D]).then_inc(o2_steps, 1)
                    dve.wait_ge(o2_steps, b.count(4, 2 * i + 1))
                    nc.vector.tensor_tensor(o2[:, i, :].rearrange("p (h m) -> p h m", h=H), heads[:, :, 0:D],
                                            rden2[i][:, :].unsqueeze(2).to_broadcast([P, H, D]), ALU.mult).then_inc(o2_steps, 1)

            def residual2(b, _):
                dve.wait_ge(pe_o, b.count(1, 1))
                dve.wait_ge(parked[b.par], b.pair(16, 16))
                nc.vector.tensor_tensor(x2[:, :, :], ffn_bank[1][:, 0:S].rearrange("p (t c) -> p t c", t=T),
                                        x1_parked[b.par][:, :, :], ALU.add).then_inc(x2_done, 1)

            def choose_experts(b, _):
                step = [0]

                def follow(ins):
                    step[0] += 1
                    ins.then_inc(route, 1)
                    dve.wait_ge(route, b.count(ROUTE, step[0]))

                def per_tile(v):
                    return v[:, :].rearrange("p (t e) -> p t e", t=T)

                def bc(v):
                    return v[:, :].unsqueeze(2).to_broadcast([P, T, E])

                dve.wait_ge(tanr_done, b.count(1, 1))
                dve.wait_ge(bias_in, 32)
                dve.wait_ge(consts, N_CONSTS)
                follow(nc.vector.tensor_scalar(sig[:, :], tanr[:, :], 0.5, 0.5, ALU.mult, ALU.add))
                follow(nc.vector.tensor_tensor(per_tile(biased), per_tile(sig),
                                               rbias_all[:, :].unsqueeze(1).to_broadcast([P, T, E]), ALU.add))
                for pick in (pick1, pick2):
                    follow(nc.vector.tensor_reduce(top[:, :], per_tile(biased), AX.X, ALU.max))
                    follow(nc.vector.tensor_tensor(per_tile(is_top), per_tile(biased), bc(top), ALU.is_ge))
                    follow(nc.vector.tensor_tensor(rank[:, :], is_top[:, :], first_rank[:, :], ALU.mult))
                    follow(nc.vector.tensor_reduce(top[:, :], per_tile(rank), AX.X, ALU.max))
                    follow(nc.vector.tensor_tensor(per_tile(pick), per_tile(rank), bc(top), ALU.is_equal))
                    if pick is pick1:
                        follow(nc.vector.scalar_tensor_tensor(out=biased[:, :], in0=pick[:, :], scalar=-1e30,
                                                              in1=biased[:, :], op0=ALU.mult, op1=ALU.add))
                follow(nc.vector.tensor_tensor(pick1[:, :], pick1[:, :], pick2[:, :], ALU.add))
                follow(nc.vector.tensor_tensor(wsel[:, :], sig[:, :], pick1[:, :], ALU.mult))
                follow(nc.vector.tensor_reduce(wsum[:, :], per_tile(wsel), AX.X, ALU.add))
                follow(nc.vector.tensor_scalar(wsum[:, :], wsum[:, :], 1e-9, None, ALU.add))
                follow(nc.vector.reciprocal(top[:, :], wsum[:, :]))
                follow(nc.vector.tensor_tensor(per_tile(cw), per_tile(wsel), bc(top), ALU.mult))
                assert step[0] == ROUTE, step

            def gate(b, _):
                dve.wait_ge(tang_done, b.count(1, 1))
                nc.vector.scalar_tensor_tensor(out=gated[:, :], in0=tang[:, :], scalar=1.0, in1=ffn_bank[0][:, :],
                                               op0=ALU.add, op1=ALU.mult).then_inc(gated_done, 1)

            def times_up(b, _):
                dve.wait_ge(pe_up, b.count(1, 1))
                dve.wait_ge(gated_done, b.count(1, 1))
                nc.vector.tensor_tensor(hid0[:, :], gated[:, :], ffn_bank[1][:, :], ALU.mult).then_inc(hid0_done, 1)

            def skip_experts(b, _):
                v = cw[:, :].rearrange("p (t e) -> p t e", t=T)
                nc.vector.tensor_tensor(cskip[:, :], v[:, :, EM], v[:, :, EM + 2], ALU.add).then_inc(cskip_done, 1)
                dve.wait_ge(cskip_done, b.count(1, 1))
                for i in range(T):
                    nc.vector.scalar_tensor_tensor(out=skip[:, i, :], in0=norm[3]["out"][:, i, :], scalar=cskip[:, i:i + 1],
                                                   in1=x2[:, i, :], op0=ALU.mult, op1=ALU.add).then_inc(skip_done, 1)

            def finish(b, _):
                dve.wait_ge(pe_down, b.count(1, 1))
                dve.wait_ge(base_done, b.count(1, 1))
                dve.wait_ge(out_stored, b.count(16, 1))
                nc.vector.tensor_tensor(result[:, :, :], ffn_bank[1][:, 0:S].rearrange("p (t c) -> p t c", t=T),
                                        base[:, :, :], ALU.add).then_inc(result_done, 1)

            rounds(dve, {"clear": clear_stacks, "norm1": stats(1), "norm2": stats(2), "norm3": stats(3), "self_q1": phi_q, "self_kv": phi_k,
                         "self_sum": mask_kvsum, "self_out": divide_out1, "self_proj": residual1,
                         "self_q2": remainder("q", scale), "self_k": remainder("k", 1.0), "max": reduce_scores,
                         "maxrow": max_mid, "ffn_out_t": divide_out2, "ffn_o": residual2, "ffn_router": choose_experts,
                         "ffn_gate": gate, "ffn_up": times_up, "ffn_cw": skip_experts, "ffn_down": finish})

        @block.tensor
        def _(pe):
            def mm(out, lhsT, rhs, start=True, stop=True):
                return nc.tensor.matmul(out, lhsT, rhs, start=start, stop=stop, skip_group_check=True)

            def two_transposes(bank, source):
                for i in range(T):
                    ins = nc.tensor.transpose(bank[:, i * P:(i + 1) * P], source[:, i, :], ident[:, :])
                return ins

            pe.wait_ge(consts, N_CONSTS)
            pe.wait_ge(weights_in, 16)

            def self_x_t(b, _):
                pe.wait_ge(xn_done[1], b.count(2, 2))
                if b.since(1):
                    pe.wait_ge(rest_done["k"], b.count(1))
                if b.since(2):
                    pe.wait_ge(vs_done, b.count(1, -1))
                two_transposes(self_bank, norm[1]["out"]).then_inc(pe_x_t, 1)

            def self_q1(b, _):
                pe.wait_ge(xnT_done, b.count(1, 1))
                mm(self_bank[:, 0:S], w["qkv"][:, 0:C], xnT[:, :]).then_inc(pe_q1, 1)

            def self_kv(b, _):
                pe.wait_ge(q_act, b.count(2, 2))
                for i in range(T):
                    ins = mm(self_bank[:, i * 2 * C:(i + 1) * 2 * C], xnT[:, i * P:(i + 1) * P], w["qkv"][:, C:3 * C])
                ins.then_inc(pe_kv, 1)

            def self_sum(b, _):
                pe.wait_ge(phik_done, b.count(1, 1))
                pe.wait_ge(k_act, b.count(3, 3))
                for i in range(T):
                    ins = mm(self_bank[:, 0:C + 1], phik[:, i, :], vones[:, i, :], start=i == 0, stop=i == T - 1)
                ins.then_inc(pe_sum, 1)

            def self_out(b, _):
                pe.wait_ge(kvsum_done, b.count(2, 2))
                pe.wait_ge(phiq_done, b.count(1, 1))
                for i in range(T):
                    ins = mm(self_bank[:, i * (C + H):(i + 1) * (C + H)], phiq[:, i * P:(i + 1) * P], kvsum[:, :])
                ins.then_inc(pe_out1, 1)

            def self_o_t(b, _):
                pe.wait_ge(o1_steps, b.count(3, 3))
                two_transposes(self_bank, o1).then_inc(pe_o_t, 1)

            def self_proj(b, _):
                pe.wait_ge(o1T_done, b.count(1, 1))
                for i in range(T):
                    ins = mm(self_bank[:, i * C:(i + 1) * C], o1T[:, i * P:(i + 1) * P], w["proj"])
                ins.then_inc(pe_proj, 1)

            def self_norm_t(b, _):
                pe.wait_ge(xn_done[2], b.count(2, 2))
                two_transposes(self_bank, norm[2]["out"]).then_inc(pe_norm_t, 1)

            def self_q2(b, _):
                pe.wait_ge(x2nT_done, b.count(1, 1))
                mm(self_bank[:, 0:S], w["q"], x2nT[:, :]).then_inc(pe_q2, 1)

            def self_k(b, _):
                pe.wait_ge(rest_done["q"], b.count(1, 1))
                pe.wait_ge(ctx_in[b.par], b.pair(16, 16))
                mm(self_bank[:, 0:S], w["k"], ctxin[b.par][:, :]).then_inc(pe_k, 1)

            def self_v(b, _):
                if b.c + 1 < B or not isinstance(b.trip, int):
                    pe.wait_ge(rest_done["k"], b.count(1, 2))
                pe.wait_ge(ctx_in[b.par], b.pair(16, 16))
                for i in range(T):
                    ins = mm(self_bank[:, i * C:(i + 1) * C], ctxin[b.par][:, i * P:(i + 1) * P], w["v"])
                ins.then_inc(pe_v, 1)

            def max_scores(b, u):
                g, k = divmod(u, 3)
                half = g // 2
                n = u + half
                if n >= 2 or b.since(1):
                    pe.wait_ge(max_read, b.count(MAX_UNITS, n - 1))
                if u in (0, 6):
                    pe.wait_ge(stack_in[half], b.count(STACK_IN, STACK_IN))
                q, kk, bank = qs[b.par], ks[b.par], max_bank[n % 2]
                if k == 0:
                    mm(bank[:, :], identb[:, :], causal[:, :], stop=False)
                    for j in range(4):
                        ins = mm(bank[:, j * P:(j + 1) * P], q[:, 4 * g + j, 0:P], kk[:, 4 * g + j, 0:P], start=False)
                else:
                    mm(group_view(bank, 2)[:, :, P:S], identb[:, :], group_view(causal, 4)[:, 0:2, :], stop=False)
                    for j in range(2):
                        h = 4 * g + 2 * (k - 1) + j
                        for i in range(T):
                            ins = mm(bank[:, j * S + i * P:j * S + (i + 1) * P], q[:, h, P:S], kk[:, h, i * P:(i + 1) * P], start=False)
                ins.then_inc(pe_max, 1)

            def maxrow(b, half):
                k = 6 if half == 0 else 13
                pe.wait_ge(max_read, b.count(MAX_UNITS, k))
                nc.tensor.transpose(max_bank[k % 2][0:T * HALF, 0:P], negmax[:, half, :, :].rearrange("p h t -> p (h t)"),
                                    ident[:, :]).then_inc(pe_maxrow, 1)

            def soft_scores(b, u):
                g, k = divmod(u, 3)
                if u >= 2 or b.since(1):
                    pe.wait_ge(exp_done, b.count(EXP_UNITS, u - 1))
                if u in (0, 6):
                    pe.wait_ge(max_in[u // 6], b.count(32, 32))
                q, kk, bank = qs[b.par], ks[b.par], soft_bank[u % 2]
                if k < 2:
                    for j in range(2):
                        h = 4 * g + 2 * k + j
                        ins = mm(bank[:, j * S:(j + 1) * S], kk[:, h, 0:P], q[:, h, :])
                else:
                    for j in range(4):
                        h = 4 * g + j
                        ins = mm(bank[:, j * P:(j + 1) * P], kk[:, h, P:S], q[:, h, P:S])
                ins.then_inc(pe_soft, 1)

            def pv(b, g):
                pe.wait_ge(masked, b.count(EXP_UNITS, 3 * g + 3))
                if g == 0:
                    pe.wait_ge(vs_done, b.count(1, 1))
                if g >= 1 or b.since(1):
                    pe.wait_ge(outT_done, b.count(4, g))
                p = probs[g % 2]
                for i in range(T):
                    for j in range(4):
                        rhs = p[:, j // 2, (j % 2) * S:(j % 2) * S + S] if i == 0 else p[:, 2, j * P:(j + 1) * P]
                        ins = mm(pv_bank[VW * j:VW * j + VW, i * P:S], vs[b.par][:, i, 4 * g + j, :], rhs,
                                 start=i == 0, stop=i == T - 1)
                ins.then_inc(pe_pv, 1)

            def ffn_out_t(b, _):
                pe.wait_ge(outT_done, b.count(4, 4))
                pe.wait_ge(result_done, b.count(1, 1))
                for i in range(T):
                    for g in range(4):
                        ins = nc.tensor.transpose(ffn_bank[i][:, g * P:(g + 1) * P], outT[:, g, i * P:(i + 1) * P], ident[:, :])
                    ins.then_inc(pe_out_t, 1)

            def ffn_o2_t(b, _):
                pe.wait_ge(o2_steps, b.count(4, 4))
                two_transposes(ffn_bank[0], o2).then_inc(pe_o2_t, 1)

            def ffn_o(b, _):
                pe.wait_ge(o2T_done, b.count(1, 1))
                for i in range(T):
                    ins = mm(ffn_bank[1][:, i * C:(i + 1) * C], o2T[:, i * P:(i + 1) * P], w["o"])
                ins.then_inc(pe_o, 1)

            def ffn_x_t(b, _):
                pe.wait_ge(xn_done[3], b.count(2, 2))
                two_transposes(ffn_bank[0], norm[3]["out"]).then_inc(pe_ffn_x_t, 1)

            def ffn_router(b, _):
                pe.wait_ge(x3T_done, b.count(1, 1))
                for i in range(T):
                    ins = mm(ffn_bank[1][:, i * E:(i + 1) * E], x3T[:, KC - 1 + i * P:KC - 1 + (i + 1) * P], w["router"])
                ins.then_inc(pe_router, 1)

            def expert_pairs(bank, weights):
                for i in range(2):
                    ins = mm(bank[:, i * S:(i + 1) * S], weights[:, i * P:(i + 1) * P], x3T[:, KC - 1:KC - 1 + S])
                return ins

            def ffn_gate(b, _):
                expert_pairs(ffn_bank[0], w["gate"]).then_inc(pe_gate, 1)

            def ffn_up(b, _):
                pe.wait_ge(tanr_done, b.count(1, 1))
                expert_pairs(ffn_bank[1], w["up"]).then_inc(pe_up, 1)

            def ffn_cw(b, _):
                pe.wait_ge(cw_wide_done, b.count(1, 1))
                pe.wait_ge(gated_done, b.count(1, 1))
                for i in range(2):
                    for t in range(T):
                        ins = nc.tensor.transpose(ffn_bank[0][:, i * S + t * P:i * S + (t + 1) * P],
                                                  cw_wide[:, t, i * P:(i + 1) * P], ident[:, :])
                ins.then_inc(pe_cw, 1)

            def ffn_down(b, _):
                pe.wait_ge(hid_done, b.count(1, 1))
                pe.wait_ge(conv_steps, b.count(CONV, CONV))
                for t in range(T):
                    o = ffn_bank[1][:, t * C:(t + 1) * C]
                    for i in range(2):
                        mm(o, hid[:, i * S + t * P:i * S + (t + 1) * P], w["down"][:, i * C:(i + 1) * C], start=i == 0, stop=False)
                    ins = mm(o, conv[:, t * P:(t + 1) * P], ident[:, :], start=False)
                ins.then_inc(pe_down, 1)

            rounds(pe, {f.__name__: f for f in (self_x_t, self_q1, self_kv, self_sum, self_out, self_o_t, self_proj, self_norm_t,
                                                self_q2, self_k, self_v, maxrow, pv, ffn_out_t, ffn_o2_t, ffn_o, ffn_x_t,
                                                ffn_router, ffn_gate, ffn_up, ffn_cw, ffn_down)}
                   | {"max": max_scores, "soft": soft_scores})


def kernel(**inputs):
    import concourse.bacc as bacc
    from concourse.bass_utils import run_bass_kernel_spmd

    a = {n: np.ascontiguousarray(v) for n, v in inputs.items()}

    def dims_first(v):
        return v.reshape(2, HALF, D, C).transpose(0, 2, 1, 3).reshape(C, C)

    pieces = {
        "qkv": a["L0_attn_Wqkv"].T, "proj": a["L0_attn_Wproj"].T,
        "q": dims_first(a["L0_xattn_Wq"]).T, "k": dims_first(a["L0_xattn_Wk"]).T, "v": a["L0_xattn_Wv"].T, "o": a["L0_xattn_Wo"].T,
        "gate": a["L0_ffn_Wg"].transpose(1, 0, 2).reshape(C, EM * I),
        "up": a["L0_ffn_Wu"].transpose(1, 0, 2).reshape(C, EM * I),
        "down": a["L0_ffn_Wd"].reshape(2, P, C).transpose(1, 0, 2).reshape(P, 2 * C),
        "router": a["L0_ffn_Wr"], "conv": a["L0_ffn_conv_w"].reshape(KC, C).T,
        "conv_b": a["L0_ffn_conv_b"].reshape(C, 1),
    }
    arrays = {
        "x": a["x"],
        "ctxT": np.ascontiguousarray(a["ctx_1024"].reshape(B * S, C).T),
        "weights": np.ascontiguousarray(np.concatenate([pieces[n] for n, _ in WEIGHTS], axis=1)),
        "bproj": a["L0_attn_bproj"],
        "router_bias": a["L0_ffn_router_bias"],
    }
    nc = bacc.Bacc("TRN2", target_bir_lowering=False, num_devices=1)
    args = {n: nc.dram_tensor(f"{n}_dram", v.shape, mybir.dt.from_np(v.dtype), kind="ExternalInput").ap()
            for n, v in arrays.items()}
    out = nc.dram_tensor("out_dram", (B, S, C), mybir.dt.float32, kind="ExternalOutput").ap()
    build(nc, out=out, **args)
    r = run_bass_kernel_spmd(nc, [{f"{n}_dram": v for n, v in arrays.items()}], core_ids=[0])
    return r.results[0]["out_dram"]
```

```python
import numpy as np
import concourse.bass as bass
from concourse import mybir
from contextlib import ExitStack

B, S, C, H, D = 8, 256, 128, 16, 8
E, EM, I = 8, 4, 64
KC = 4
P = 128
T = S // P
HALF = H // 2
MAX_ROW = 64
STACK = 96
EXP_UNITS = 12
MAX_UNITS = 14
BF16_ONES = float(np.array([0x3F803F80], np.uint32).view(np.float32)[0])
NOTHING, PICKED = -3e30, 1e30
VW = 32

WEIGHTS = [("qkv", 3 * C), ("proj", C), ("q", C), ("k", C), ("v", C), ("o", C), ("gate", EM * I),
           ("up", EM * I), ("down", 2 * C), ("router", E), ("conv", KC), ("conv_b", 1)]

ORDER = {
    "sp": [
        ("park", 1, 0), ("load", 3, 0), ("load_ctx", 3, 0), ("stack_k", 1, 1), ("stack_q", 1, 1), ("zero_max", 2, 0),
        ("send_max", 1, 0), ("store_k", 2, 0), ("store_q", 2, 0), ("stack_k", 2, 0), ("stack_q", 2, 0),
        ("send_max", 1, 1), ("store_out", -1, 0),
    ],
    "pool": [
        ("conv", -1, 0), ("mask", 0, 9), ("rstd2", 2, 0), ("mask", 0, 10), ("mask", 0, 11), ("rstd1", 3, 0),
        ("bias", 3, 0), ("lo_k", 2, 0), ("lo_q", 2, 0), ("mask", 1, 0), ("hid", -1, 0), ("hid", -1, 1),
        ("mask", 1, 1), ("base", -1, 0), ("mask", 1, 2), ("mask", 1, 3), ("rstd3", 0, 0), ("mask", 1, 4),
        ("mask", 1, 5), ("mask", 1, 6), ("mask", 1, 7), ("mask", 1, 8),
    ],
    "act": [
        ("exp", 0, 10), ("tanh_r", -1, 0), ("hi_k", 2, 0), ("exp", 0, 11), ("outT", 0, 2), ("max_hi", 1, 0),
        ("norm2", 2, 0), ("tanh_g", -1, 0), ("vs", 2, 0), ("mid_k", 2, 0), ("outT", 0, 3), ("x2nT", 2, 0),
        ("norm1", 3, 0), ("hi_q", 2, 0), ("widen", -1, 0), ("mid_q", 2, 0), ("relu7", -1, 0), ("xnT", 3, 0),
        ("exp", 1, 0), ("cwT", -1, 0), ("act_q", 3, 0), ("exp", 1, 1), ("exp", 1, 2), ("act_kv", 3, 0),
        ("max_hi", 1, 1), ("o2T", 0, 0), ("exp", 1, 3), ("exp", 1, 4), ("exp", 1, 5), ("outT", 1, 0), ("o1T", 3, 0),
        ("exp", 1, 6), ("norm3", 0, 0), ("exp", 1, 7), ("exp", 1, 8), ("x3T", 0, 0), ("exp", 1, 9), ("outT", 1, 1),
    ],
    "dve": [
        ("reduce", 1, 4), ("var2", 2, 1), ("reduce", 1, 5), ("tap", -1, 0), ("route", -1, 0), ("rest_k", 2, 0),
        ("shift2", 2, 0), ("clear", 2, 5), ("route", -1, 1), ("clear", 3, 0), ("clear", 3, 1), ("stats1", 3, 0),
        ("route", -1, 2), ("route", -1, 3), ("route", -1, 4), ("var1", 3, 0), ("route", -1, 5), ("max_mid", 1, 0),
        ("route", -1, 6), ("route", -1, 7), ("route", -1, 8), ("var1", 3, 1), ("route", -1, 9), ("gate", -1, 0),
        ("reduce", 1, 6), ("shift1", 3, 0), ("clear", 3, 2), ("clear", 3, 3), ("reduce", 1, 7), ("times_up", -1, 0),
        ("rest_q", 2, 0), ("clear", 2, 6), ("div2", 0, 0), ("skip", -1, 0), ("div2", 0, 1), ("reduce", 1, 8),
        ("reduce", 1, 9), ("tap", -1, 1), ("div2", 0, 2), ("reduce", 1, 10), ("reduce", 1, 11), ("div2", 0, 3),
        ("tap", -1, 2), ("phi_q", 3, 0), ("skip", -1, 1), ("phi_k", 3, 0), ("max_mid", 1, 1), ("finish", -1, 0),
        ("kvsum", 3, 0), ("x2", 0, 0), ("stats3", 0, 0), ("var3", 0, 0), ("div1", 3, 0), ("var3", 0, 1),
        ("div1", 3, 1), ("div1", 3, 2), ("reduce", 2, 0), ("reduce", 2, 1), ("shift3", 0, 0), ("reduce", 2, 2),
        ("x1", 3, 0), ("reduce", 2, 3), ("stats2", 3, 0), ("var2", 3, 0),
    ],
    "pe": [
        ("soft", 0, 10), ("self_k", 2, 0), ("max", 1, 5), ("ffn_router", -1, 0), ("soft", 0, 11), ("pv", 0, 2),
        ("maxrow", 1, 0), ("ffn_gate", -1, 0), ("self_v", 2, 0), ("pv", 0, 3), ("max", 1, 6), ("max", 1, 7),
        ("self_norm_t", 2, 0), ("ffn_up", -1, 0), ("self_q2", 2, 0), ("ffn_out_t", 0, 0), ("max", 1, 8),
        ("max", 1, 9), ("self_x_t", 3, 0), ("soft", 1, 0), ("ffn_cw", -1, 0), ("ffn_out_t", 0, 1), ("self_q1", 3, 0),
        ("max", 1, 10), ("max", 1, 11), ("soft", 1, 1), ("soft", 1, 2), ("self_kv", 3, 0), ("maxrow", 1, 1),
        ("soft", 1, 3), ("ffn_o2_t", 0, 0), ("ffn_down", -1, 0), ("self_sum", 3, 0), ("ffn_o", 0, 0), ("soft", 1, 4),
        ("soft", 1, 5), ("self_out", 3, 0), ("pv", 1, 0), ("max", 2, 0), ("max", 2, 1), ("self_o_t", 3, 0),
        ("soft", 1, 6), ("soft", 1, 7), ("max", 2, 2), ("self_proj", 3, 0), ("max", 2, 3), ("soft", 1, 8),
        ("pv", 1, 1), ("ffn_x_t", 0, 0), ("soft", 1, 9), ("max", 2, 4),
    ],
}
FIRST_ROUND, LAST_ROUND = -3, B
LOOP_FROM, LOOP_TRIPS = 1, 2


class Batch:

    def __init__(self, trip, c):
        self.trip, self.c = trip, c
        self.par = c % 2

    def count(self, per, plus=0):
        assert per * self.c + plus >= (0 if isinstance(self.trip, int) else 1)
        return self.trip * (2 * per) + (per * self.c + plus)

    def pair(self, per, plus=0):
        assert per * (self.c // 2) + plus >= 0
        return self.trip * per + (per * (self.c // 2) + plus)

    def since(self, n):
        assert isinstance(self.trip, int) or self.c >= n
        return self.c >= n

    @property
    def number(self):
        return self.trip * 2 + self.c if self.c else self.trip * 2


def rounds(engine, name, steps):
    def one(trip, r):
        for step, off, arg in ORDER[name]:
            in_loop = LOOP_FROM <= r < LOOP_FROM + 2 * LOOP_TRIPS
            if in_loop or 0 <= r + off < B:
                steps[step](Batch(trip, r + off), arg)

    r = FIRST_ROUND
    while r <= LAST_ROUND:
        if r == LOOP_FROM:
            with engine.Fori(0, LOOP_TRIPS) as trip:
                one(trip, r)
                one(trip, r + 1)
            r += 2 * LOOP_TRIPS
        else:
            one(0, r)
            r += 1


def build(nc, x, ctxT, weights, bproj, router_bias, out):
    f32, bf16 = mybir.dt.float32, mybir.dt.bfloat16
    ALU, ACT, AX = mybir.AluOpType, mybir.ActivationFunctionType, mybir.AxisListType
    scale = float(D) ** -0.5

    ctx = ExitStack()
    with ctx:
        def sb(name, shape, dt=f32):
            return ctx.enter_context(nc.sbuf_tensor(name, shape, dt))

        def pb(name):
            return ctx.enter_context(nc.psum_tensor(name, [P, 512], f32))

        def sem(name):
            return ctx.enter_context(nc.semaphore(name))

        ctx.enter_context(nc.allow_non_contiguous_dma(reason="rows of 512 bytes"))
        ctx.enter_context(nc.allow_low_precision(reason="exact splits into bfloat16 parts"))

        parts_dram = {n: nc.dram_tensor(f"{n}_parts", [2, 3, 2, D, HALF, S], bf16, kind="Internal").ap()
                      for n in "qk"}

        W = sb("W", [P, sum(n for _, n in WEIGHTS)])
        w, at = {}, 0
        for name, n in WEIGHTS:
            w[name] = W[:, at:at + n]
            at += n
        bproj_all = sb("bproj_all", [P, C])
        rbias_all = sb("rbias_all", [P, E])
        ident = sb("ident", [P, P])
        identb = sb("identb", [P, P], bf16)
        causal = sb("causal", [P, 512], bf16)
        headmask = sb("headmask", [P, C])
        headsel = sb("headsel", [P, H])
        exponent = sb("exponent", [P, T])

        xin = [sb(f"xin{i}", [P, T, C]) for i in range(2)]
        ctxin = [sb(f"ctxin{i}", [C, S]) for i in range(2)]
        norm = {}
        for n in (1, 2, 3):
            norm[n] = dict(stats=sb(f"stats{n}", [P, T, 6]), mv=sb(f"mv{n}", [P, T, 2]),
                           vareps=sb(f"vareps{n}", [P, T]),
                           rstd=sb(f"rstd{n}", [P, T]), shift=sb(f"shift{n}", [P, T]),
                           out=sb(f"xn{n}", [P, T, C]))
        xnT = sb("xnT", [C, S])
        expq, reluq, phiq = sb("expq", [C, S]), sb("reluq", [C, S]), sb("phiq", [C, S])
        expk, reluk, phik = sb("expk", [P, T, C]), sb("reluk", [P, T, C]), sb("phik", [P, T, C])
        vones = sb("vones", [P, T, C + 1])
        kvsum = sb("kvsum", [C, C + H])
        den1, rden1 = sb("den1", [P, T, H]), sb("rden1", [P, T, H])
        o1, o1T = sb("o1", [P, T, C]), sb("o1T", [C, S])
        xres = sb("xres", [P, T, C])
        x1 = [sb(f"x1_{i}", [P, T, C]) for i in range(2)]
        x1_parked = [sb(f"x1_parked{i}", [P, T, C]) for i in range(2)]
        x2nT = sb("x2nT", [C, S])
        parts = {n: sb(f"{n}parts", [C, 3, S], bf16) for n in "qk"}
        rest = {n: sb(f"{n}rest", [C, S]) for n in "qk"}
        qs = [sb(f"qs{i}", [STACK, H, S], bf16) for i in range(2)]
        ks = [sb(f"ks{i}", [STACK, H, S], bf16) for i in range(2)]
        vs = [sb(f"vs{i}", [P, T, H, VW]) for i in range(2)]
        negmax = sb("negmax", [P, 2, HALF, T])
        maxparts = [sb(f"maxparts{i}", [T * HALF, 2, P], bf16) for i in range(2)]
        probs = [sb(f"probs{i}", [P, 3, 512]) for i in range(2)]
        outT = sb("outT", [P, 4, S])
        rden2 = [sb(f"rden2_{i}", [P, H]) for i in range(2)]
        o2, o2T = sb("o2", [P, T, C]), sb("o2T", [C, S])
        x2 = sb("x2", [P, T, C])
        x3T = sb("x3T", [C, KC - 1 + S])
        tanr, sig = sb("tanr", [P, T * E]), sb("sig", [P, T * E])
        biased, picked = sb("biased", [P, T, E + 6]), sb("picked", [P, T, E + 6])
        best, match = sb("best", [P, T, 8]), sb("match", [P, T, 8])
        wsel, wsum, rwsum, cw = sb("wsel", [P, T * E]), sb("wsum", [P, T]), sb("rwsum", [P, T]), sb("cw", [P, T * E])
        cskip = sb("cskip", [P, T])
        cw_wide = sb("cw_wide", [P, T, EM * I])
        tang, gated, hid0, hid, cwT = (sb(n, [P, 2 * S]) for n in ("tang", "gated", "hid0", "hid", "cwT"))
        conv = sb("conv", [C, S])
        relu7, skip, base = sb("relu7", [P, T, C]), sb("skip", [P, T, C]), sb("base", [P, T, C])
        result = sb("result", [P, T, C])

        soft_bank = [pb(f"soft_bank{i}") for i in range(2)]
        max_bank = [pb(f"max_bank{i}") for i in range(2)]
        pv_bank, self_bank = pb("pv_bank"), pb("self_bank")
        ffn_bank = [pb(f"ffn_bank{i}") for i in range(2)]

        qkv_in = sem("qkv_in")
        weights_in, bias_in, rbias_in, consts, cleared = sem("weights_in"), sem("bias_in"), sem("rbias_in"), sem("consts"), sem("cleared")
        x_in = [sem(f"x_in{i}") for i in range(2)]
        ctx_in = [sem(f"ctx_in{i}") for i in range(2)]
        stats_done = {n: sem(f"stats_done{n}") for n in norm}
        mv_done = {n: sem(f"mv_done{n}") for n in norm}
        vareps_done = {n: sem(f"vareps_done{n}") for n in norm}
        rstd_done = {n: sem(f"rstd_done{n}") for n in norm}
        shift_done = {n: sem(f"shift_done{n}") for n in norm}
        xn_done = {n: sem(f"xn_done{n}") for n in norm}
        pe_x_t, pe_q1, pe_kv, pe_sum, pe_out1, pe_o_t, pe_proj = (
            sem(n) for n in ("pe_x_t", "pe_q1", "pe_kv", "pe_sum", "pe_out1", "pe_o_t", "pe_proj"))
        pe_norm_t, pe_q2, pe_k, pe_v = (sem(n) for n in ("pe_norm_t", "pe_q2", "pe_k", "pe_v"))
        xnT_done, q_act, k_act = sem("xnT_done"), sem("q_act"), sem("k_act")
        phiq_done, phik_done, kvsum_done = sem("phiq_done"), sem("phik_done"), sem("kvsum_done")
        o1_steps, o1T_done, xres_done, x1_done = (
            sem(n) for n in ("o1_steps", "o1T_done", "xres_done", "x1_done"))
        x2nT_done = sem("x2nT_done")
        hi_done, mid_done, rest_done, rest2_done, lo_done = (
            {n: sem(f"{n}_{s}") for n in "qk"} for s in ("hi_done", "mid_done", "rest_done", "rest2_done", "lo_done"))
        stored = {n: sem(f"{n}_stored") for n in "qk"}
        stack_in = [[sem(f"stack_in{i}{j}") for j in range(2)] for i in range(2)]
        zero_in = [sem(f"zero_in{i}") for i in range(2)]
        max_in = [sem(f"max_in{i}") for i in range(2)]
        vs_done, parked = sem("vs_done"), [sem(f"parked{i}") for i in range(2)]
        pe_soft, exp_done, masked = sem("pe_soft"), sem("exp_done"), sem("masked")
        pe_max, max_read = sem("pe_max"), sem("max_read")
        pe_maxrow, maxhi_done = sem("pe_maxrow"), sem("maxhi_done")
        pe_pv, outT_done = sem("pe_pv"), sem("outT_done")
        pe_out_t, o2_steps = sem("pe_out_t"), sem("o2_steps")
        pe_o2_t, o2T_done, pe_o, x2_done, pe_ffn_x_t, x3T_done = (
            sem(n) for n in ("pe_o2_t", "o2T_done", "pe_o", "x2_done", "pe_ffn_x_t", "x3T_done"))
        pe_router, tanr_done, route = sem("pe_router"), sem("tanr_done"), sem("route")
        pe_gate, tang_done, gated_done, pe_up, hid0_done, pe_cw, cwT_done, hid_done, pe_down = (
            sem(n) for n in ("pe_gate", "tang_done", "gated_done", "pe_up", "hid0_done", "pe_cw",
                             "cwT_done", "hid_done", "pe_down"))
        conv_steps, relu7_done, skip_done, base_done, result_done, out_stored = (
            sem(n) for n in ("conv_steps", "relu7_done", "skip_done", "base_done", "result_done", "out_stored"))
        cskip_done, cw_wide_done = sem("cskip_done"), sem("cw_wide_done")
        WARM_START, WARM_STEP = 11, 2
        ROUTE = 12
        N_CONSTS = 7 + 5 + 2 + 5
        CLEARED_0, CLEARED = 4, 6
        STACK_IN = 16 * 6

        block = ctx.enter_context(nc.Block())

        def all_clear(b):
            return CLEARED if b.since(1) else CLEARED_0

        def settle(engine, *counts):
            for count in counts:
                if not isinstance(count, int):
                    engine.lower_val(count)
            engine.wait_ge(consts, 1)

        def group_view(bank, n):
            return bank[:, 0:512].rearrange("p (n c) -> p n c", n=n)

        @block.sync
        def _(sp):
            x_v = x.rearrange("b (t p) c -> b p t c", p=P)
            out_v = out.rearrange("b (t p) c -> b p t c", p=P)
            ctx_v = ctxT.rearrange("c (b s) -> b c s", s=S)

            def load_x(b):
                sp.dma_start(xin[b.par][:, :, :], x_v[b.number]).then_inc(x_in[b.par], 16)

            def load_ctx(b):
                sp.dma_start(ctxin[b.par][:, :], ctx_v[b.number]).then_inc(ctx_in[b.par], 16)

            load_x(Batch(0, 0))
            for part, arrived in ((slice(0, 3 * C), qkv_in), (slice(3 * C, None), weights_in)):
                sp.dma_start(W[:, part], weights[:, part]).then_inc(arrived, 16)
            sp.dma_start(bproj_all[:, :], bproj.unsqueeze(0).to_broadcast([P, C])).then_inc(bias_in, 16)
            load_x(Batch(0, 1))
            load_ctx(Batch(0, 0))
            load_ctx(Batch(0, 1))
            sp.dma_start(rbias_all[:, :], router_bias.unsqueeze(0).to_broadcast([P, E])).then_inc(rbias_in, 16)

            def load(b, _):
                if b.since(2):
                    reached = b.count(1, -1)
                    settle(sp, reached)
                    sp.wait_ge(x1_done, reached)
                    load_x(b)

            def load_context(b, _):
                if b.since(2):
                    reached = b.count(1, -1)
                    settle(sp, reached)
                    sp.wait_ge(vs_done, reached)
                    load_ctx(b)

            def store_parts(n):
                def go(b, _):
                    lo, read = b.count(1, 1), b.pair(STACK_IN)
                    settle(sp, lo, read)
                    if b.since(2):
                        for half in range(2):
                            sp.wait_ge(stack_in[b.par][half], read)
                    sp.wait_ge(lo_done[n], lo)
                    sp.dma_start(parts_dram[n][b.par].rearrange("part u d h s -> (u d h) part s"),
                                 parts[n][:, :, :]).then_inc(stored[n], 16)
                return go

            def heads_of(half):
                return slice(HALF * half, HALF * half + HALF)

            def stack(n, orders):
                def go(b, half):
                    all_stored = b.count(16, 16)
                    softened = b.count(EXP_UNITS, -2 * EXP_UNITS + 6 * (half + 1)) if b.since(2) else 0
                    settle(sp, all_stored, softened)
                    sp.wait_ge(cleared, all_clear(b))
                    sp.wait_ge(stored[n], all_stored)
                    if b.since(2):
                        sp.wait_ge(pe_soft, softened)
                    rows = parts_dram[n][b.par, :, half].rearrange("part d h s -> part d (h s)")
                    tile = {"q": qs, "k": ks}[n][b.par]
                    at = 0
                    for first, n_parts, times in orders:
                        source = rows[first:first + n_parts]
                        if times > 1:
                            source = source.to_broadcast([times, D, HALF * S])
                        n_rows = n_parts * times * D
                        sp.dma_start(tile[at:at + n_rows, heads_of(half), :].rearrange("r h s -> r (h s)"),
                                     source).then_inc(stack_in[b.par][half], 16)
                        at += n_rows
                return go

            def zero_max(b, _):
                if b.since(2):
                    softened = b.count(EXP_UNITS, -EXP_UNITS)
                    settle(sp, softened)
                    sp.wait_ge(pe_soft, softened)
                sp.wait_ge(cleared, all_clear(b))
                sp.dma_start(qs[b.par][MAX_ROW:MAX_ROW + 2, :, :].rearrange("r h s -> r (h s)"),
                             qs[b.par][MAX_ROW + 2:MAX_ROW + 4, :, :].rearrange("r h s -> r (h s)")).then_inc(zero_in[b.par], 16)

            def send_max(b, half):
                ready = b.count(MAX_UNITS, 7 * (half + 1))
                settle(sp, ready)
                sp.wait_ge(max_read, ready)
                for part in range(2):
                    row = qs[b.par][MAX_ROW + part:MAX_ROW + part + 1, heads_of(half), :]
                    sp.dma_start(row.rearrange("r h (t q) -> r (h t) q", t=T),
                                 maxparts[half][:, part, :]).then_inc(max_in[half], 16)

            def park(b, _):
                written, read = b.count(1, 1), b.count(1, -1) if b.since(2) else 0
                settle(sp, written, read)
                if b.since(2):
                    sp.wait_ge(x2_done, read)
                sp.wait_ge(x1_done, written)
                sp.dma_start(x1_parked[b.par][:, :, :], x1[b.par][:, :, :]).then_inc(parked[b.par], 16)

            def store_out(b, _):
                reached = b.count(1, 2)
                settle(sp, reached)
                sp.wait_ge(result_done, reached)
                sp.dma_start(out_v[b.number], result[:, :, :]).then_inc(out_stored, 16)

            rounds(sp, "sp", {"load": load, "load_ctx": load_context, "store_q": store_parts("q"), "store_k": store_parts("k"),
                              "stack_q": stack("q", [(0, 1, 3), (1, 1, 2), (2, 1, 1)]),
                              "stack_k": stack("k", [(0, 3, 1), (0, 2, 1), (0, 1, 1)]),
                              "zero_max": zero_max, "send_max": send_max, "park": park, "store_out": store_out})
            sp.wait_ge(out_stored, 16 * B + 1)

        @block.gpsimd
        def _(pool):
            def const(ins):
                ins.then_inc(consts, 1)

            nc.gpsimd.memset(result[:, :, :], 0.0).then_inc(result_done, 1)
            nc.gpsimd.memset(wsum[:, :], 0.0).then_inc(out_stored, 1)
            const(nc.gpsimd.memset(exponent[:, :], -0.5))
            const(nc.gpsimd.memset(ident[:, :], 0.0))
            const(nc.gpsimd.memset(headmask[:, :], 1.0))
            const(nc.gpsimd.memset(headsel[:, :], 1.0))
            const(nc.gpsimd.memset(vones[:, :, C:C + 1], 1.0))
            const(nc.gpsimd.memset(causal[:, :], 0.0))
            const(nc.gpsimd.memset(identb[:, :], 0.0))
            pool.wait_ge(consts, 7)
            const(nc.gpsimd.affine_select(out=ident[:, :], in_=ident[:, :], compare_op=ALU.not_equal, fill=1.0,
                                          base=0, pattern=[[-1, P]], channel_multiplier=1))

            def other_consts():
                const(nc.gpsimd.affine_select(out=identb[:, :], in_=identb[:, :], compare_op=ALU.not_equal, fill=1.0,
                                              base=0, pattern=[[-1, P]], channel_multiplier=1))
                const(nc.gpsimd.affine_select(out=group_view(causal, 4), in_=group_view(causal, 4), compare_op=ALU.is_ge,
                                              fill=-1e30, base=0, pattern=[[0, 4], [-1, P]], channel_multiplier=1))
                for tile, pat in ((headmask[:, :].rearrange("p (h m) -> p h m", h=H), [[-D, H], [0, D]]),
                                  (headsel[:, :], [[-D, H]])):
                    const(nc.gpsimd.affine_select(out=tile, in_=tile, compare_op=ALU.is_ge, fill=0.0,
                                                  base=0, pattern=pat, channel_multiplier=1))
                pool.wait_ge(consts, 12)
                for tile, pat in ((headmask[:, :].rearrange("p (h m) -> p h m", h=H), [[D, H], [0, D]]),
                                  (headsel[:, :], [[D, H]])):
                    const(nc.gpsimd.affine_select(out=tile, in_=tile, compare_op=ALU.is_ge, fill=0.0,
                                                  base=D - 1, pattern=pat, channel_multiplier=-1))
                const(nc.gpsimd.memset(biased[:, :, E:E + 6], NOTHING))
                const(nc.gpsimd.memset(match[:, :, 2:8], NOTHING))
                const(nc.gpsimd.memset(x3T[:, 0:KC - 1], 0.0))
                const(nc.gpsimd.memset(vs[1][:, :, :, :], 0.0))
                pool.wait_ge(consts, N_CONSTS - 1)
                const(nc.gpsimd.memset(vs[1][:, :, :, D], 1.0))

            def rstd(n):
                t = norm[n]

                def go(b, _):
                    pool.wait_ge(vareps_done[n], b.count(1, 1))
                    if n != 3 and b.since(1):
                        pool.wait_ge(xn_done[n], b.count(2))
                    nc.gpsimd.tensor_tensor(t["rstd"][:, :], t["vareps"][:, :], exponent[:, :], ALU.pow).then_inc(rstd_done[n], 1)
                    if n == 1 and not b.since(1):
                        other_consts()
                return go

            def add_bias(b, _):
                pool.wait_ge(x_in[b.par], b.pair(16, 16))
                pool.wait_ge(bias_in, 16)
                if b.since(1):
                    pool.wait_ge(x1_done, b.count(1))
                nc.gpsimd.tensor_tensor(xres[:, :, :], xin[b.par][:, :, :],
                                        bproj_all[:, :].unsqueeze(1).to_broadcast([P, T, C]), ALU.add).then_inc(xres_done, 1)

            def lowest_part(n):
                def go(b, _):
                    pool.wait_ge(mid_done[n], b.count(1, 1))
                    if b.since(1):
                        pool.wait_ge(stored[n], b.count(16))
                    nc.gpsimd.tensor_tensor(parts[n][:, 2, :], rest[n][:, :], parts[n][:, 1, :], ALU.subtract).then_inc(lo_done[n], 1)
                return go

            def mask_probs(b, u):
                g, k = divmod(u, 3)
                ready = b.count(EXP_UNITS, u + 1)
                settle(pool, ready)
                pool.wait_ge(exp_done, ready)
                n = 4 if k == 2 else 2
                v = probs[g % 2][:, k, :].rearrange("p (n q) -> p n q", n=n)[:, :, 0:P]
                nc.gpsimd.affine_select(out=v, in_=v, compare_op=ALU.is_ge, fill=0.0, base=0,
                                        pattern=[[0, n], [1, P]], channel_multiplier=-1).then_inc(masked, 1)

            def convolve(b, _):
                ready = b.count(1, 1)
                settle(pool, ready)
                pool.wait_ge(x3T_done, ready)
                pool.wait_ge(weights_in, 16)
                nc.gpsimd.tensor_scalar(conv[:, :], x3T[:, KC - 1:KC - 1 + S], w["conv"][:, KC - 1:KC], w["conv_b"],
                                        ALU.mult, ALU.add).then_inc(conv_steps, 1)

            def weigh_hidden(b, i):
                pool.wait_ge(hid0_done, b.count(1, 1))
                pool.wait_ge(cwT_done, b.count(1, 1))
                at = slice(i * S, (i + 1) * S)
                nc.gpsimd.tensor_tensor(hid[:, at], hid0[:, at], cwT[:, at], ALU.mult).then_inc(hid_done, 1)

            def add_base(b, _):
                pool.wait_ge(relu7_done, b.count(2, 2))
                pool.wait_ge(skip_done, b.count(2, 2))
                nc.gpsimd.tensor_tensor(base[:, :, :], skip[:, :, :], relu7[:, :, :], ALU.add).then_inc(base_done, 1)

            rounds(pool, "pool", {"rstd1": rstd(1), "rstd2": rstd(2), "rstd3": rstd(3), "bias": add_bias,
                                  "lo_q": lowest_part("q"), "lo_k": lowest_part("k"), "mask": mask_probs,
                                  "conv": convolve, "hid": weigh_hidden, "base": add_base})

        @block.scalar
        def _(act):
            def normalise(n):
                t = norm[n]

                def go(b, _):
                    act.wait_ge(shift_done[n], b.count(1, 1))
                    source = {1: xin[b.par], 2: x1[b.par], 3: x2}[n]
                    if n == 1:
                        act.wait_ge(x_in[b.par], b.pair(16, 16))
                    if n != 3 and b.since(1):
                        act.wait_ge({1: pe_x_t, 2: pe_norm_t}[n], b.count(1))
                    for i in range(T):
                        nc.scalar.activation(t["out"][:, i, :], source[:, i, :], ACT.Identity,
                                             scale=t["rstd"][:, i:i + 1], bias=t["shift"][:, i:i + 1]).then_inc(xn_done[n], 1)
                return go

            def copy_xnT(b, _):
                act.wait_ge(pe_x_t, b.count(1, 1))
                if b.since(1):
                    act.wait_ge(pe_kv, b.count(1))
                nc.scalar.copy(xnT[:, :], self_bank[:, 0:S]).then_inc(xnT_done, 1)

            def act_q(b, _):
                act.wait_ge(pe_q1, b.count(1, 1))
                if b.since(1):
                    act.wait_ge(phiq_done, b.count(1))
                nc.scalar.activation(expq[:, :], self_bank[:, 0:S], ACT.Exp).then_inc(q_act, 1)
                nc.scalar.activation(reluq[:, :], self_bank[:, 0:S], ACT.Relu).then_inc(q_act, 1)

            def act_kv(b, _):
                act.wait_ge(pe_kv, b.count(1, 1))
                if b.since(1):
                    act.wait_ge(phik_done, b.count(1))
                    act.wait_ge(pe_sum, b.count(1))
                kv = group_view(self_bank, T)
                nc.scalar.activation(expk[:, :, :], kv[:, :, 0:C], ACT.Exp).then_inc(k_act, 1)
                nc.scalar.activation(reluk[:, :, :], kv[:, :, 0:C], ACT.Relu).then_inc(k_act, 1)
                nc.scalar.copy(vones[:, :, 0:C], kv[:, :, C:2 * C]).then_inc(k_act, 1)

            def copy_o1T(b, _):
                act.wait_ge(pe_o_t, b.count(1, 1))
                if b.since(1):
                    act.wait_ge(pe_proj, b.count(1))
                nc.scalar.copy(o1T[:, :], self_bank[:, 0:S]).then_inc(o1T_done, 1)

            def copy_x2nT(b, _):
                act.wait_ge(pe_norm_t, b.count(1, 1))
                if b.since(1):
                    act.wait_ge(pe_q2, b.count(1))
                nc.scalar.copy(x2nT[:, :], self_bank[:, 0:S]).then_inc(x2nT_done, 1)

            def high_part(n, pe_done, factor):
                def go(b, _):
                    act.wait_ge(pe_done, b.count(1, 1))
                    if b.since(1):
                        act.wait_ge(stored[n], b.count(16))
                    nc.scalar.mul(parts[n][:, 0, :], self_bank[:, 0:S], factor).then_inc(hi_done[n], 1)
                return go

            def middle_part(n):
                def go(b, _):
                    act.wait_ge(rest_done[n], b.count(1, 1))
                    nc.scalar.copy(parts[n][:, 1, :], rest[n][:, :]).then_inc(mid_done[n], 1)
                return go

            def copy_v(b, _):
                act.wait_ge(pe_v, b.count(1, 1))
                act.wait_ge(cleared, all_clear(b))
                act.wait_ge(consts, N_CONSTS)
                if b.since(2):
                    act.wait_ge(pe_pv, b.count(4, -4))
                nc.scalar.copy(vs[b.par][:, :, :, 0:D], self_bank[:, 0:S].rearrange("p (t h d) -> p t h d", t=T, h=H)).then_inc(vs_done, 1)

            def exp_scores(b, u):
                g, k = divmod(u, 3)
                act.wait_ge(pe_soft, b.count(EXP_UNITS, u + 1))
                if g >= 2 or b.since(1):
                    act.wait_ge(pe_pv, b.count(4, g - 1))
                nc.scalar.activation(probs[g % 2][:, k, :], soft_bank[u % 2][:, :], ACT.Exp).then_inc(exp_done, 1)

            def max_high(b, half):
                act.wait_ge(pe_maxrow, b.count(2, half + 1))
                if b.since(1):
                    act.wait_ge(max_in[half], b.count(32))
                k = 6 if half == 0 else 13
                nc.scalar.copy(maxparts[half][:, 0, :], max_bank[k % 2][0:T * HALF, 0:P]).then_inc(maxhi_done, 1)

            def copy_outT(b, g):
                act.wait_ge(pe_pv, b.count(4, g + 1))
                if g == 0 and b.since(1):
                    act.wait_ge(pe_out_t, b.count(2))
                nc.scalar.copy(outT[:, g, :], pv_bank[:, 0:S]).then_inc(outT_done, 1)

            def copy_o2T(b, _):
                act.wait_ge(pe_o2_t, b.count(1, 1))
                nc.scalar.copy(o2T[:, :], pv_bank[:, 0:S]).then_inc(o2T_done, 1)

            def copy_x3T(b, _):
                act.wait_ge(pe_ffn_x_t, b.count(1, 1))
                nc.scalar.copy(x3T[:, KC - 1:KC - 1 + S], ffn_bank[0][:, 0:S]).then_inc(x3T_done, 1)

            def tanh_router(b, _):
                act.wait_ge(pe_router, b.count(1, 1))
                nc.scalar.activation(tanr[:, :], ffn_bank[1][:, 0:T * E], ACT.Tanh, scale=0.5).then_inc(tanr_done, 1)

            def tanh_gate(b, _):
                act.wait_ge(pe_gate, b.count(1, 1))
                nc.scalar.activation(tang[:, :], ffn_bank[0][:, :], ACT.Tanh, scale=0.5).then_inc(tang_done, 1)

            def widen_cw(b, _):
                act.wait_ge(route, b.count(ROUTE, ROUTE))
                nc.scalar.activation(cw_wide[:, :, :].rearrange("p t (e i) -> p t e i", e=EM),
                                     cw[:, :].rearrange("p (t e) -> p t e", t=T)[:, :, 0:EM].unsqueeze(3).to_broadcast([P, T, EM, I]),
                                     ACT.Copy, scale=0.5).then_inc(cw_wide_done, 1)

            def relu_expert(b, _):
                act.wait_ge(route, b.count(ROUTE, ROUTE))
                for i in range(T):
                    nc.scalar.activation(relu7[:, i, :], norm[3]["out"][:, i, :], ACT.Relu,
                                         scale=cw[:, i * E + 7:i * E + 8]).then_inc(relu7_done, 1)

            def copy_cwT(b, _):
                act.wait_ge(pe_cw, b.count(1, 1))
                nc.scalar.copy(cwT[:, :], ffn_bank[0][:, :]).then_inc(cwT_done, 1)

            rounds(act, "act", {"norm1": normalise(1), "norm2": normalise(2), "norm3": normalise(3), "xnT": copy_xnT,
                                "act_q": act_q, "act_kv": act_kv, "o1T": copy_o1T, "x2nT": copy_x2nT,
                                "hi_q": high_part("q", pe_q2, scale), "mid_q": middle_part("q"),
                                "hi_k": high_part("k", pe_k, 1.0), "mid_k": middle_part("k"), "vs": copy_v,
                                "exp": exp_scores, "max_hi": max_high, "outT": copy_outT, "o2T": copy_o2T,
                                "x3T": copy_x3T, "tanh_r": tanh_router, "tanh_g": tanh_gate, "widen": widen_cw,
                                "relu7": relu_expert, "cwT": copy_cwT})

        @block.vector
        def _(dve):
            def clear(b, part):
                if b.since(1):
                    return
                par, what = divmod(part, 4)
                if what == 0:
                    ins = nc.vector.memset(vs[par][:, :, :, :], 0.0)
                elif what == 1:
                    ins = nc.vector.memset(ks[par][:, :, :].rearrange("r h s -> r (h s)").bitcast(f32), BF16_ONES)
                elif what == 2:
                    ins = nc.vector.memset(qs[par][:, :, :].rearrange("r h s -> r (h s)").bitcast(f32), 0.0)
                else:
                    dve.wait_ge(cleared, 1)
                    ins = nc.vector.memset(vs[par][:, :, :, D], 1.0)
                ins.then_inc(cleared, 1)

            def stats(n):
                t = norm[n]

                def go(b, _):
                    source = {1: xin[b.par], 2: x1[b.par], 3: x2}[n]
                    if n == 1:
                        dve.wait_ge(x_in[b.par], b.pair(16, 16))
                    else:
                        dve.wait_ge({2: x1_done, 3: x2_done}[n], b.count(1, 1))
                    if n != 3 and b.since(1):
                        dve.wait_ge(shift_done[n], b.count(1))
                    for i in range(T):
                        nc.vector.bn_stats(t["stats"][:, i, :], source[:, i, :]).then_inc(stats_done[n], 1)
                return go

            def variance(n):
                t = norm[n]

                def go(b, i):
                    if i == 0:
                        ready = b.count(2, 2)
                        settle(dve, ready)
                        dve.wait_ge(stats_done[n], ready)
                        for i in range(T):
                            nc.vector.bn_aggr(t["mv"][:, i, :], t["stats"][:, i, :]).then_inc(mv_done[n], 1)
                    else:
                        dve.wait_ge(mv_done[n], b.count(2, 2))
                        nc.vector.tensor_scalar(t["vareps"][:, :], t["mv"][:, :, 1], 1e-5, None, ALU.add).then_inc(vareps_done[n], 1)
                return go

            def shift(n):
                t = norm[n]

                def go(b, _):
                    dve.wait_ge(rstd_done[n], b.count(1, 1))
                    if n != 3 and b.since(1):
                        dve.wait_ge(xn_done[n], b.count(2))
                    nc.vector.scalar_tensor_tensor(out=t["shift"][:, :], in0=t["mv"][:, :, 0], scalar=-1.0, in1=t["rstd"][:, :],
                                                   op0=ALU.mult, op1=ALU.mult).then_inc(shift_done[n], 1)
                return go

            def phi_q(b, _):
                dve.wait_ge(q_act, b.count(2, 2))
                if b.since(1):
                    dve.wait_ge(pe_out1, b.count(1))
                nc.vector.scalar_tensor_tensor(out=phiq[:, :], in0=expq[:, :], scalar=1.0, in1=reluq[:, :],
                                               op0=ALU.min, op1=ALU.add).then_inc(phiq_done, 1)

            def phi_k(b, _):
                dve.wait_ge(k_act, b.count(3, 2))
                if b.since(1):
                    dve.wait_ge(pe_sum, b.count(1))
                nc.vector.scalar_tensor_tensor(out=phik[:, :, :], in0=expk[:, :, :], scalar=1.0, in1=reluk[:, :, :],
                                               op0=ALU.min, op1=ALU.add).then_inc(phik_done, 1)

            def mask_kvsum(b, _):
                dve.wait_ge(pe_sum, b.count(1, 1))
                dve.wait_ge(consts, N_CONSTS)
                if b.since(1):
                    dve.wait_ge(pe_out1, b.count(1))
                nc.vector.tensor_tensor(kvsum[:, 0:C], self_bank[:, 0:C], headmask[:, :], ALU.mult).then_inc(kvsum_done, 1)
                nc.vector.tensor_scalar(kvsum[:, C:C + H], headsel[:, :], self_bank[:, C:C + 1], None, ALU.mult).then_inc(kvsum_done, 1)

            def divide_out1(b, i):
                both = self_bank[:, 0:T * (C + H)].rearrange("p (t c) -> p t c", t=T)
                if i == 0:
                    dve.wait_ge(pe_out1, b.count(1, 1))
                    nc.vector.tensor_scalar(den1[:, :, :], both[:, :, C:C + H], 1e-6, None, ALU.add).then_inc(o1_steps, 1)
                elif i == 1:
                    dve.wait_ge(o1_steps, b.count(3, 1))
                    nc.vector.reciprocal(rden1[:, :, :], den1[:, :, :]).then_inc(o1_steps, 1)
                else:
                    dve.wait_ge(o1_steps, b.count(3, 2))
                    if b.since(1):
                        dve.wait_ge(pe_o_t, b.count(1))
                    for t in range(T):
                        ins = nc.vector.tensor_tensor(o1[:, t, :].rearrange("p (h m) -> p h m", h=H),
                                                      both[:, t, 0:C].rearrange("p (h m) -> p h m", h=H),
                                                      rden1[:, t, :].unsqueeze(2).to_broadcast([P, H, D]), ALU.mult)
                    ins.then_inc(o1_steps, 1)

            def residual1(b, _):
                dve.wait_ge(pe_proj, b.count(1, 1))
                dve.wait_ge(xres_done, b.count(1, 1))
                if b.since(2):
                    dve.wait_ge(parked[b.par], b.pair(16))
                    dve.wait_ge(xn_done[2], b.count(2, -2))
                nc.vector.tensor_tensor(x1[b.par][:, :, :], self_bank[:, 0:S].rearrange("p (t c) -> p t c", t=T),
                                        xres[:, :, :], ALU.add).then_inc(x1_done, 1)

            def remainder(n, factor):
                def go(b, _):
                    dve.wait_ge(hi_done[n], b.count(1, 1))
                    if b.since(1):
                        dve.wait_ge(lo_done[n], b.count(1))
                    nc.vector.scalar_tensor_tensor(out=rest[n][:, :], in0=self_bank[:, 0:S], scalar=factor,
                                                   in1=parts[n][:, 0, :], op0=ALU.mult, op1=ALU.subtract).then_inc(rest_done[n], 1)
                return go

            def reduce_scores(b, u):
                g, k = divmod(u, 3)
                half = g // 2
                dve.wait_ge(pe_max, b.count(EXP_UNITS, u + 1))
                if b.since(1):
                    dve.wait_ge(pe_maxrow, b.count(2, half - 1))
                at, n = (4 * (g % 2), 4) if k == 0 else (4 * (g % 2) + 2 * (k - 1), 2)
                nc.vector.tensor_reduce(negmax[:, half, at:at + n, min(k, 1)], group_view(max_bank[(u + half) % 2], n),
                                        AX.X, ALU.max, negate=True).then_inc(max_read, 1)

            def max_mid(b, half):
                dve.wait_ge(maxhi_done, b.count(2, half + 1))
                if b.since(1):
                    dve.wait_ge(max_in[half], b.count(32))
                k = 6 if half == 0 else 13
                nc.vector.tensor_tensor(maxparts[half][:, 1, :], max_bank[k % 2][0:T * HALF, 0:P],
                                        maxparts[half][:, 0, :], ALU.subtract).then_inc(max_read, 1)

            def divide_out2(b, k):
                i, product = divmod(k, 2)
                heads = pv_bank[:, :].rearrange("p (h m) -> p h m", h=H)
                if not product:
                    dve.wait_ge(pe_out_t, b.count(2, i + 1))
                    nc.vector.reciprocal(rden2[i][:, :], heads[:, :, D]).then_inc(o2_steps, 1)
                else:
                    dve.wait_ge(o2_steps, b.count(4, 2 * i + 1))
                    nc.vector.tensor_tensor(o2[:, i, :].rearrange("p (h m) -> p h m", h=H), heads[:, :, 0:D],
                                            rden2[i][:, :].unsqueeze(2).to_broadcast([P, H, D]), ALU.mult).then_inc(o2_steps, 1)

            def residual2(b, _):
                dve.wait_ge(pe_o, b.count(1, 1))
                dve.wait_ge(parked[b.par], b.pair(16, 16))
                dve.wait_ge(result_done, b.count(1, 1))
                nc.vector.tensor_tensor(x2[:, :, :], pv_bank[:, 0:S].rearrange("p (t c) -> p t c", t=T),
                                        x1_parked[b.par][:, :, :], ALU.add).then_inc(x2_done, 1)

            def choose_experts(b, i):
                def per_tile(v):
                    return v[:, :].rearrange("p (t e) -> p t e", t=T)

                if i == 0:
                    dve.wait_ge(tanr_done, b.count(1, 1))
                    nc.vector.tensor_scalar(sig[:, :], tanr[:, :], 0.5, 0.5, ALU.mult, ALU.add).then_inc(route, 1)
                    return
                before = b.count(ROUTE, [0, 1, 2, 4, 5, 7, 8, 9, 10, 11][i])
                settle(dve, before)
                dve.wait_ge(route, before)
                if i == 1:
                    dve.wait_ge(rbias_in, 16)
                    dve.wait_ge(consts, N_CONSTS)
                    nc.vector.tensor_tensor(biased[:, :, 0:E], per_tile(sig),
                                            rbias_all[:, :].unsqueeze(1).to_broadcast([P, T, E]), ALU.add).then_inc(route, 1)
                elif i == 2:
                    for t in range(T):
                        nc.vector.max(best[:, t, :], biased[:, t, 0:E]).then_inc(route, 1)
                elif i == 3:
                    nc.vector.tensor_copy(match[:, :, 0:2], best[:, :, 0:2]).then_inc(route, 1)
                elif i == 4:
                    for t in range(T):
                        nc.vector.match_replace(picked[:, t, :], match[:, t, :], biased[:, t, :], PICKED).then_inc(route, 1)
                elif i == 5:
                    nc.vector.scalar_tensor_tensor(out=per_tile(wsel), in0=picked[:, :, 0:E], scalar=PICKED, in1=per_tile(sig),
                                                   op0=ALU.is_ge, op1=ALU.mult).then_inc(route, 1)
                elif i == 6:
                    nc.vector.tensor_reduce(wsum[:, :], per_tile(wsel), AX.X, ALU.add).then_inc(route, 1)
                elif i == 7:
                    nc.vector.tensor_scalar(wsum[:, :], wsum[:, :], 1e-9, None, ALU.add).then_inc(route, 1)
                elif i == 8:
                    nc.vector.reciprocal(rwsum[:, :], wsum[:, :]).then_inc(route, 1)
                elif i == 9:
                    nc.vector.tensor_tensor(per_tile(cw), per_tile(wsel), rwsum[:, :].unsqueeze(2).to_broadcast([P, T, E]),
                                            ALU.mult).then_inc(route, 1)

            def gate(b, _):
                dve.wait_ge(tang_done, b.count(1, 1))
                nc.vector.scalar_tensor_tensor(out=gated[:, :], in0=tang[:, :], scalar=1.0, in1=ffn_bank[0][:, :],
                                               op0=ALU.add, op1=ALU.mult).then_inc(gated_done, 1)

            def times_up(b, _):
                dve.wait_ge(pe_up, b.count(1, 1))
                dve.wait_ge(gated_done, b.count(1, 1))
                nc.vector.tensor_tensor(hid0[:, :], gated[:, :], ffn_bank[1][:, :], ALU.mult).then_inc(hid0_done, 1)

            def skip_experts(b, i):
                v = cw[:, :].rearrange("p (t e) -> p t e", t=T)
                if i == 0:
                    dve.wait_ge(route, b.count(ROUTE, ROUTE))
                    nc.vector.tensor_tensor(cskip[:, :], v[:, :, EM], v[:, :, EM + 2], ALU.add).then_inc(cskip_done, 1)
                else:
                    dve.wait_ge(cskip_done, b.count(1, 1))
                    for t in range(T):
                        nc.vector.scalar_tensor_tensor(out=skip[:, t, :], in0=norm[3]["out"][:, t, :], scalar=cskip[:, t:t + 1],
                                                       in1=x2[:, t, :], op0=ALU.mult, op1=ALU.add).then_inc(skip_done, 1)

            def add_tap(b, j):
                dve.wait_ge(conv_steps, b.count(KC, j + 1))
                nc.vector.scalar_tensor_tensor(out=conv[:, :], in0=x3T[:, j:j + S], scalar=w["conv"][:, j:j + 1],
                                               in1=conv[:, :], op0=ALU.mult, op1=ALU.add).then_inc(conv_steps, 1)

            def finish(b, _):
                dve.wait_ge(pe_down, b.count(1, 1))
                dve.wait_ge(base_done, b.count(1, 1))
                dve.wait_ge(out_stored, b.count(16, 1))
                nc.vector.tensor_tensor(result[:, :, :], ffn_bank[1][:, 0:S].rearrange("p (t c) -> p t c", t=T),
                                        base[:, :, :], ALU.add).then_inc(result_done, 1)

            rounds(dve, "dve", {"clear": clear, "stats1": stats(1), "stats2": stats(2), "stats3": stats(3),
                                "var1": variance(1), "var2": variance(2), "var3": variance(3),
                                "shift1": shift(1), "shift2": shift(2), "shift3": shift(3), "phi_q": phi_q, "phi_k": phi_k,
                                "kvsum": mask_kvsum, "div1": divide_out1, "x1": residual1,
                                "rest_q": remainder("q", scale), "rest_k": remainder("k", 1.0), "reduce": reduce_scores,
                                "max_mid": max_mid, "div2": divide_out2, "x2": residual2, "route": choose_experts,
                                "gate": gate, "times_up": times_up, "skip": skip_experts, "tap": add_tap, "finish": finish})

        @block.tensor
        def _(pe):
            def mm(out, lhsT, rhs, start=True, stop=True):
                return nc.tensor.matmul(out, lhsT, rhs, start=start, stop=stop, skip_group_check=True)

            def two_transposes(bank, source):
                for i in range(T):
                    ins = nc.tensor.transpose(bank[:, i * P:(i + 1) * P], source[:, i, :], ident[:, :])
                return ins

            def keep_warm(name, step, n):
                early = 1
                if ("self_" + name, 3, 0) in ORDER["pe"] and all(off <= 1 for s, off, _ in ORDER["pe"] if s == "soft"):
                    early = 2

                def go(b, arg):
                    step(b, arg)
                    if b.c < early and isinstance(b.trip, int):
                        for _ in range(n):
                            mm(soft_bank[0][:, 0:P], ident[:, :], ident[:, :])
                return go

            pe.wait_ge(consts, 8)
            keep_warm("", lambda b, _: None, WARM_START)(Batch(0, 0), 0)

            def self_x_t(b, _):
                pe.wait_ge(xn_done[1], b.count(2, 2))
                if b.since(1):
                    pe.wait_ge(rest_done["q"], b.count(1))
                two_transposes(self_bank, norm[1]["out"]).then_inc(pe_x_t, 1)

            def self_q1(b, _):
                pe.wait_ge(xnT_done, b.count(1, 1))
                pe.wait_ge(qkv_in, 16)
                mm(self_bank[:, 0:S], w["qkv"][:, 0:C], xnT[:, :]).then_inc(pe_q1, 1)

            def self_kv(b, _):
                pe.wait_ge(q_act, b.count(2, 2))
                for i in range(T):
                    ins = mm(self_bank[:, i * 2 * C:(i + 1) * 2 * C], xnT[:, i * P:(i + 1) * P], w["qkv"][:, C:3 * C])
                ins.then_inc(pe_kv, 1)

            def self_sum(b, _):
                pe.wait_ge(phik_done, b.count(1, 1))
                pe.wait_ge(k_act, b.count(3, 3))
                for i in range(T):
                    ins = mm(self_bank[:, 0:C + 1], phik[:, i, :], vones[:, i, :], start=i == 0, stop=i == T - 1)
                ins.then_inc(pe_sum, 1)

            def self_out(b, _):
                pe.wait_ge(kvsum_done, b.count(2, 2))
                pe.wait_ge(phiq_done, b.count(1, 1))
                for i in range(T):
                    ins = mm(self_bank[:, i * (C + H):(i + 1) * (C + H)], phiq[:, i * P:(i + 1) * P], kvsum[:, :])
                ins.then_inc(pe_out1, 1)

            def self_o_t(b, _):
                pe.wait_ge(o1_steps, b.count(3, 3))
                two_transposes(self_bank, o1).then_inc(pe_o_t, 1)

            def self_proj(b, _):
                pe.wait_ge(o1T_done, b.count(1, 1))
                pe.wait_ge(weights_in, 16)
                for i in range(T):
                    ins = mm(self_bank[:, i * C:(i + 1) * C], o1T[:, i * P:(i + 1) * P], w["proj"])
                ins.then_inc(pe_proj, 1)

            def self_norm_t(b, _):
                pe.wait_ge(xn_done[2], b.count(2, 2))
                pe.wait_ge(vs_done, b.count(1, 1))
                two_transposes(self_bank, norm[2]["out"]).then_inc(pe_norm_t, 1)

            def self_q2(b, _):
                pe.wait_ge(x2nT_done, b.count(1, 1))
                mm(self_bank[:, 0:S], w["q"], x2nT[:, :]).then_inc(pe_q2, 1)

            def self_k(b, _):
                pe.wait_ge(x1_done, b.count(1, 1))
                pe.wait_ge(ctx_in[b.par], b.pair(16, 16))
                mm(self_bank[:, 0:S], w["k"], ctxin[b.par][:, :]).then_inc(pe_k, 1)

            def self_v(b, _):
                pe.wait_ge(rest_done["k"], b.count(1, 1))
                pe.wait_ge(ctx_in[b.par], b.pair(16, 16))
                for i in range(T):
                    ins = mm(self_bank[:, i * C:(i + 1) * C], ctxin[b.par][:, i * P:(i + 1) * P], w["v"])
                ins.then_inc(pe_v, 1)

            def max_scores(b, u):
                g, k = divmod(u, 3)
                half = g // 2
                n = u + half
                if n >= 2 or b.since(1):
                    pe.wait_ge(max_read, b.count(MAX_UNITS, n - 1))
                if u in (0, 6):
                    pe.wait_ge(consts, N_CONSTS)
                    pe.wait_ge(stack_in[b.par][half], b.pair(STACK_IN, STACK_IN))
                    pe.wait_ge(zero_in[b.par], b.pair(16, 16))
                q, kk, bank = qs[b.par], ks[b.par], max_bank[n % 2]
                if k == 0:
                    mm(bank[:, :], identb[:, :], causal[:, :], stop=False)
                    for j in range(4):
                        ins = mm(bank[:, j * P:(j + 1) * P], q[:, 4 * g + j, 0:P], kk[:, 4 * g + j, 0:P], start=False)
                else:
                    mm(group_view(bank, 2)[:, :, P:S], identb[:, :], group_view(causal, 4)[:, 0:2, :], stop=False)
                    for j in range(2):
                        h = 4 * g + 2 * (k - 1) + j
                        for i in range(T):
                            ins = mm(bank[:, j * S + i * P:j * S + (i + 1) * P], q[:, h, P:S], kk[:, h, i * P:(i + 1) * P], start=False)
                ins.then_inc(pe_max, 1)

            def maxrow(b, half):
                k = 6 if half == 0 else 13
                pe.wait_ge(max_read, b.count(MAX_UNITS, k))
                nc.tensor.transpose(max_bank[k % 2][0:T * HALF, 0:P], negmax[:, half, :, :].rearrange("p h t -> p (h t)"),
                                    ident[:, :]).then_inc(pe_maxrow, 1)

            def soft_scores(b, u):
                g, k = divmod(u, 3)
                if u >= 2 or b.since(1):
                    pe.wait_ge(exp_done, b.count(EXP_UNITS, u - 1))
                if u in (0, 6):
                    pe.wait_ge(max_in[u // 6], b.count(32, 32))
                q, kk, bank = qs[b.par], ks[b.par], soft_bank[u % 2]
                if k < 2:
                    for j in range(2):
                        h = 4 * g + 2 * k + j
                        ins = mm(bank[:, j * S:(j + 1) * S], kk[:, h, 0:P], q[:, h, :])
                else:
                    for j in range(4):
                        h = 4 * g + j
                        ins = mm(bank[:, j * P:(j + 1) * P], kk[:, h, P:S], q[:, h, P:S])
                ins.then_inc(pe_soft, 1)

            def pv(b, g):
                pe.wait_ge(masked, b.count(EXP_UNITS, 3 * g + 3))
                if g == 0:
                    pe.wait_ge(vs_done, b.count(1, 1))
                if g >= 1:
                    pe.wait_ge(outT_done, b.count(4, g))
                elif b.since(1):
                    pe.wait_ge(x2_done, b.count(1))
                p = probs[g % 2]
                for i in range(T):
                    for j in range(4):
                        rhs = p[:, j // 2, (j % 2) * S:(j % 2) * S + S] if i == 0 else p[:, 2, j * P:(j + 1) * P]
                        ins = mm(pv_bank[VW * j:VW * j + VW, i * P:S], vs[b.par][:, i, 4 * g + j, :], rhs,
                                 start=i == 0, stop=i == T - 1)
                ins.then_inc(pe_pv, 1)

            def ffn_out_t(b, i):
                if i == 0:
                    pe.wait_ge(outT_done, b.count(4, 4))
                else:
                    pe.wait_ge(o2_steps, b.count(4, 2))
                for g in range(4):
                    ins = nc.tensor.transpose(pv_bank[:, g * P:(g + 1) * P], outT[:, g, i * P:(i + 1) * P], ident[:, :])
                ins.then_inc(pe_out_t, 1)

            def ffn_o2_t(b, _):
                pe.wait_ge(o2_steps, b.count(4, 4))
                two_transposes(pv_bank, o2).then_inc(pe_o2_t, 1)

            def ffn_o(b, _):
                pe.wait_ge(o2T_done, b.count(1, 1))
                for i in range(T):
                    ins = mm(pv_bank[:, i * C:(i + 1) * C], o2T[:, i * P:(i + 1) * P], w["o"])
                ins.then_inc(pe_o, 1)

            def ffn_x_t(b, _):
                pe.wait_ge(xn_done[3], b.count(2, 2))
                two_transposes(ffn_bank[0], norm[3]["out"]).then_inc(pe_ffn_x_t, 1)

            def ffn_router(b, _):
                pe.wait_ge(x3T_done, b.count(1, 1))
                for i in range(T):
                    ins = mm(ffn_bank[1][:, i * E:(i + 1) * E], x3T[:, KC - 1 + i * P:KC - 1 + (i + 1) * P], w["router"])
                ins.then_inc(pe_router, 1)

            def expert_pairs(bank, weights):
                for i in range(2):
                    ins = mm(bank[:, i * S:(i + 1) * S], weights[:, i * P:(i + 1) * P], x3T[:, KC - 1:KC - 1 + S])
                return ins

            def ffn_gate(b, _):
                expert_pairs(ffn_bank[0], w["gate"]).then_inc(pe_gate, 1)

            def ffn_up(b, _):
                pe.wait_ge(tanr_done, b.count(1, 1))
                expert_pairs(ffn_bank[1], w["up"]).then_inc(pe_up, 1)

            def ffn_cw(b, _):
                pe.wait_ge(cw_wide_done, b.count(1, 1))
                pe.wait_ge(gated_done, b.count(1, 1))
                for i in range(2):
                    for t in range(T):
                        ins = nc.tensor.transpose(ffn_bank[0][:, i * S + t * P:i * S + (t + 1) * P],
                                                  cw_wide[:, t, i * P:(i + 1) * P], ident[:, :])
                ins.then_inc(pe_cw, 1)

            def ffn_down(b, _):
                pe.wait_ge(hid_done, b.count(2, 2))
                pe.wait_ge(conv_steps, b.count(KC, KC))
                for t in range(T):
                    o = ffn_bank[1][:, t * C:(t + 1) * C]
                    for i in range(2):
                        mm(o, hid[:, i * S + t * P:i * S + (t + 1) * P], w["down"][:, i * C:(i + 1) * C], start=i == 0, stop=False)
                    ins = mm(o, conv[:, t * P:(t + 1) * P], ident[:, :], start=False)
                ins.then_inc(pe_down, 1)

            self_steps = (self_x_t, self_q1, self_kv, self_sum, self_out, self_o_t, self_proj, self_norm_t, self_q2, self_k, self_v)
            other_steps = (maxrow, pv, ffn_out_t, ffn_o2_t, ffn_o, ffn_x_t, ffn_router, ffn_gate, ffn_up, ffn_cw, ffn_down)
            rounds(pe, "pe", {f.__name__: keep_warm(f.__name__[5:], f, WARM_STEP) for f in self_steps}
                   | {f.__name__: f for f in other_steps} | {"max": max_scores, "soft": soft_scores})


def kernel(**inputs):
    import concourse.bacc as bacc
    from concourse.bass_utils import run_bass_kernel_spmd

    a = {n: np.ascontiguousarray(v) for n, v in inputs.items()}

    def dims_first(v):
        return v.reshape(2, HALF, D, C).transpose(0, 2, 1, 3).reshape(C, C)

    pieces = {
        "qkv": a["L0_attn_Wqkv"].T, "proj": a["L0_attn_Wproj"].T,
        "q": dims_first(a["L0_xattn_Wq"]).T, "k": dims_first(a["L0_xattn_Wk"]).T, "v": a["L0_xattn_Wv"].T, "o": a["L0_xattn_Wo"].T,
        "gate": a["L0_ffn_Wg"].transpose(1, 0, 2).reshape(C, EM * I),
        "up": a["L0_ffn_Wu"].transpose(1, 0, 2).reshape(C, EM * I),
        "down": a["L0_ffn_Wd"].reshape(2, P, C).transpose(1, 0, 2).reshape(P, 2 * C),
        "router": a["L0_ffn_Wr"], "conv": a["L0_ffn_conv_w"].reshape(KC, C).T,
        "conv_b": a["L0_ffn_conv_b"].reshape(C, 1),
    }
    arrays = {
        "x": a["x"],
        "ctxT": np.ascontiguousarray(a["ctx_1024"].reshape(B * S, C).T),
        "weights": np.ascontiguousarray(np.concatenate([pieces[n] for n, _ in WEIGHTS], axis=1)),
        "bproj": a["L0_attn_bproj"],
        "router_bias": a["L0_ffn_router_bias"],
    }
    nc = bacc.Bacc("TRN2", target_bir_lowering=False, num_devices=1)
    args = {n: nc.dram_tensor(f"{n}_dram", v.shape, mybir.dt.from_np(v.dtype), kind="ExternalInput").ap()
            for n, v in arrays.items()}
    out = nc.dram_tensor("out_dram", (B, S, C), mybir.dt.float32, kind="ExternalOutput").ap()
    build(nc, out=out, **args)
    r = run_bass_kernel_spmd(nc, [{f"{n}_dram": v for n, v in arrays.items()}], core_ids=[0])
    return r.results[0]["out_dram"]
```
